# Optimizing a Trainium2 kernel written in Bass

```python
import numpy as np
import jax
import jax.numpy as jnp

def _softmax(x, axis=-1):
    return jax.nn.softmax(x, axis=axis)

def _gelu(x):
    return jax.nn.gelu(x, approximate=True)

def _silu(x):
    return jax.nn.silu(x)

def _sigmoid(x):
    return jax.nn.sigmoid(x)

def _layernorm(x, axis=-1, eps=1e-05):
    m = jnp.mean(x, axis=axis, keepdims=True)
    v = jnp.var(x, axis=axis, keepdims=True)
    return (x - m) / jnp.sqrt(v + eps)

def _scatter_add(tgt, idx, src, axis=0):
    return tgt.at[idx].add(src)

def _segment_sum(src, seg, n):
    return jax.ops.segment_sum(src, seg, n)
kernel_name = 'mk_decoder_preln_d1_seqx_r4_fa7541'

def setup_inputs(seed: int=0):
    np.random.seed(seed)
    _w = jnp.asarray

    def _rec_inputs():
        import jax
        import jax.numpy as jnp
        _rk = jax.random.key(seed)
        x = 6.313e-05 + 0.9998 * jax.random.normal(jax.random.fold_in(_rk, 1), (16, 256, 256), jnp.float32)
        _lenS = 256 - jax.random.randint(jax.random.fold_in(_rk, 7), (16,), 0, max(1, 256 // 4) + 1, jnp.int32)
        _lenS2 = 256 - jax.random.randint(jax.random.fold_in(_rk, 8), (16,), 0, max(1, 256 // 4) + 1, jnp.int32)
        _ctx_1024P = jax.random.normal(jax.random.fold_in(_rk, 11), (16, 16, 256), jnp.float32)
        _ctx_1024c = jax.random.dirichlet(jax.random.fold_in(_rk, 511), 0.3 * jnp.ones((16,), jnp.float32), (16, 256))
        _ctx_1024t = jnp.einsum('bsk,bkd->bsd', _ctx_1024c, _ctx_1024P)
        _ctx_1024t = _ctx_1024t * jax.lax.rsqrt(jnp.mean(jnp.square(_ctx_1024t)) + 1e-12) * 0.953939
        ctx_1024 = -0.000214406 + 1.00034 * (_ctx_1024t + 0.3 * jax.random.normal(jax.random.fold_in(_rk, 611), (16, 256, 256), jnp.float32))
        return (x, ctx_1024)
    x, ctx_1024 = _rec_inputs()

    def _L0_attn_setup():
        import jax, jax.numpy as jnp
        import numpy as np
        import math
        D_MODEL = 256
        STATE_DIM = 16
        DT_RANK = 64
        BATCH = 4
        SEQ_LEN = 256
        DT_MIN, DT_MAX = (0.001, 0.1)
        key = jax.random.key(seed)
        ks = jax.random.split(key, 6)
        x = jax.random.normal(ks[0], (BATCH, SEQ_LEN, D_MODEL), dtype=jnp.float32)
        A_log = jnp.log(jnp.broadcast_to(jnp.arange(1, STATE_DIM + 1, dtype=jnp.float32)[None, :], (D_MODEL, STATE_DIM)))
        W_delta = jax.random.uniform(ks[1], (D_MODEL, DT_RANK), minval=-1.0, maxval=1.0) * D_MODEL ** (-0.5)
        W_dt = jax.random.uniform(ks[2], (DT_RANK, D_MODEL), minval=-1.0, maxval=1.0) * DT_RANK ** (-0.5)
        b_dt = jax.random.uniform(ks[3], (D_MODEL,), minval=math.log(DT_MIN), maxval=math.log(DT_MAX))
        W_B = jax.random.uniform(ks[4], (D_MODEL, STATE_DIM), minval=-1.0, maxval=1.0) * D_MODEL ** (-0.5)
        W_C = jax.random.uniform(ks[5], (D_MODEL, STATE_DIM), minval=-1.0, maxval=1.0) * D_MODEL ** (-0.5)
        D = jnp.ones((D_MODEL,), dtype=jnp.float32)
        return {'x': x, 'A_log': A_log, 'W_delta': W_delta, 'W_dt': W_dt, 'b_dt': b_dt, 'W_B': W_B, 'W_C': W_C, 'D': D}
    _L0_attn_all = _L0_attn_setup()
    _L0_attn_in = {k: v for k, v in _L0_attn_all.items() if k in ('A_log', 'W_delta', 'W_dt', 'b_dt', 'W_B', 'W_C', 'D')}
    del _L0_attn_all

    def _L0_xattn_setup():
        import jax, jax.numpy as jnp
        import numpy as np
        from jax import lax
        BIG = jnp.float32(1e+30)

        def _pairwise_euclidean(a, b):
            aa = jnp.sum(a * a, axis=-1)[:, None]
            bb = jnp.sum(b * b, axis=-1)[None, :]
            ab = a @ b.T
            return jnp.sqrt(jnp.maximum(aa + bb - 2.0 * ab, 0.0))

        def _dtw_cost(D):
            row0 = jnp.cumsum(D[0])

            def row_step(prev_row, d_row):
                first = d_row[0] + prev_row[0]

                def col_step(left, inp):
                    d_ij, up, diag = inp
                    r = d_ij + jnp.minimum(jnp.minimum(up, left), diag)
                    return (r, r)
                _, rest = lax.scan(col_step, first, (d_row[1:], prev_row[1:], prev_row[:-1]))
                row = jnp.concatenate([first[None], rest])
                return (row, row)
            _, rows = lax.scan(row_step, row0, D[1:])
            return jnp.concatenate([row0[None], rows], axis=0)

        def _backtrack(R, T1, T2):
            L = T1 + T2 - 1

            def step(carry, _):
                i, j, done = carry
                valid = jnp.logical_not(done)
                cd = jnp.where((i > 0) & (j > 0), R[jnp.maximum(i - 1, 0), jnp.maximum(j - 1, 0)], BIG)
                cu = jnp.where(i > 0, R[jnp.maximum(i - 1, 0), j], BIG)
                cl = jnp.where(j > 0, R[i, jnp.maximum(j - 1, 0)], BIG)
                choice = jnp.argmin(jnp.stack([cd, cu, cl]))
                ni = jnp.where(choice <= 1, i - 1, i)
                nj = jnp.where((choice == 0) | (choice == 2), j - 1, j)
                at_origin = (i == 0) & (j == 0)
                ni = jnp.where(at_origin, 0, ni)
                nj = jnp.where(at_origin, 0, nj)
                return ((ni, nj, done | at_origin), (i, j, valid))
            init = (jnp.int32(T1 - 1), jnp.int32(T2 - 1), jnp.bool_(False))
            _, (i_idx, j_idx, valid) = lax.scan(step, init, None, length=L)
            return (i_idx, j_idx, valid)

        def _align_one(small, large):
            T_small, d = small.shape
            T_large = large.shape[0]
            D = _pairwise_euclidean(small, large)
            R = _dtw_cost(D)
            i_idx, j_idx, valid = _backtrack(R, T_small, T_large)
            contrib = small[i_idx] * valid[:, None].astype(small.dtype)
            expanded = jnp.zeros((T_large, d), dtype=small.dtype).at[j_idx].add(contrib)
            return expanded
        key = jax.random.key(seed)
        k1, k2 = jax.random.split(key)
        teacher = jax.random.normal(k1, (16, 100, 256), dtype=jnp.float32)
        student = jax.random.normal(k2, (16, 150, 256), dtype=jnp.float32)
        return {'teacher_features': teacher, 'student_features': student}
    _L0_xattn_all = _L0_xattn_setup()
    _L0_xattn_in = {k: v for k, v in _L0_xattn_all.items() if k in ()}
    del _L0_xattn_all

    def _L0_ffn_setup():
        import jax, jax.numpy as jnp
        import numpy as np
        NUM_EXPERTS = 64
        TOP_K = 2
        B, S, EMB, MLP = (4, 512, 256, 512)
        key = jax.random.key(seed)
        k1, k2, k3, k4, k5 = jax.random.split(key, 5)
        inputs = jax.random.normal(k1, (B, S, EMB), dtype=jnp.float32)
        gate_kernel = jax.random.normal(k2, (EMB, NUM_EXPERTS), dtype=jnp.float32) / np.sqrt(EMB)
        w0 = jax.random.normal(k3, (NUM_EXPERTS, EMB, MLP), dtype=jnp.float32) / np.sqrt(EMB)
        w1 = jax.random.normal(k4, (NUM_EXPERTS, EMB, MLP), dtype=jnp.float32) / np.sqrt(EMB)
        wo = jax.random.normal(k5, (NUM_EXPERTS, MLP, EMB), dtype=jnp.float32) / np.sqrt(MLP)
        return {'inputs': inputs, 'gate_kernel': gate_kernel, 'w0': w0, 'w1': w1, 'wo': wo}
    _L0_ffn_all = _L0_ffn_setup()
    _L0_ffn_in = {k: v for k, v in _L0_ffn_all.items() if k in ('gate_kernel', 'w0', 'w1', 'wo')}
    del _L0_ffn_all
    return {'x': x, 'ctx_1024': ctx_1024, 'L0_attn_A_log': _L0_attn_in['A_log'], 'L0_attn_W_delta': _L0_attn_in['W_delta'], 'L0_attn_W_dt': _L0_attn_in['W_dt'], 'L0_attn_b_dt': _L0_attn_in['b_dt'], 'L0_attn_W_B': _L0_attn_in['W_B'], 'L0_attn_W_C': _L0_attn_in['W_C'], 'L0_attn_D': _L0_attn_in['D'], 'L0_ffn_gate_kernel': _L0_ffn_in['gate_kernel'], 'L0_ffn_w0': _L0_ffn_in['w0'], 'L0_ffn_w1': _L0_ffn_in['w1'], 'L0_ffn_wo': _L0_ffn_in['wo']}

def reference(x, ctx_1024, L0_attn_A_log, L0_attn_W_delta, L0_attn_W_dt, L0_attn_b_dt, L0_attn_W_B, L0_attn_W_C, L0_attn_D, L0_ffn_gate_kernel, L0_ffn_w0, L0_ffn_w1, L0_ffn_wo):
    import jax
    import jax.numpy as jnp

    def _L0_attn_ref(x, A_log, W_delta, W_dt, b_dt, W_B, W_C, D):
        import jax, jax.numpy as jnp
        import numpy as np
        import math
        D_MODEL = 256
        STATE_DIM = 16
        DT_RANK = 64
        BATCH = 4
        SEQ_LEN = 256
        DT_MIN, DT_MAX = (0.001, 0.1)
        delta = jax.nn.softplus(jnp.einsum('bld,dr->blr', x, W_delta) @ W_dt + b_dt)
        Bm = jnp.einsum('bld,dn->bln', x, W_B)
        Cm = jnp.einsum('bld,dn->bln', x, W_C)
        A = -jnp.exp(A_log)
        dA = jnp.exp(delta[..., None] * A)
        dBx = delta[..., None] * Bm[:, :, None, :] * x[..., None]

        def step(h, inp):
            dA_t, dBx_t, C_t = inp
            h = dA_t * h + dBx_t
            y = jnp.einsum('bdn,bn->bd', h, C_t)
            return (h, y)
        h0 = jnp.zeros((x.shape[0], x.shape[2], A_log.shape[1]), dtype=x.dtype)
        _, ys = jax.lax.scan(step, h0, (dA.transpose(1, 0, 2, 3), dBx.transpose(1, 0, 2, 3), Cm.transpose(1, 0, 2)))
        return ys.transpose(1, 0, 2) + D * x

    def _L0_xattn_ref(teacher_features, student_features):
        import jax, jax.numpy as jnp
        import numpy as np
        from jax import lax
        BIG = jnp.float32(1e+30)

        def _pairwise_euclidean(a, b):
            aa = jnp.sum(a * a, axis=-1)[:, None]
            bb = jnp.sum(b * b, axis=-1)[None, :]
            ab = a @ b.T
            return jnp.sqrt(jnp.maximum(aa + bb - 2.0 * ab, 0.0))

        def _dtw_cost(D):
            row0 = jnp.cumsum(D[0])

            def row_step(prev_row, d_row):
                first = d_row[0] + prev_row[0]

                def col_step(left, inp):
                    d_ij, up, diag = inp
                    r = d_ij + jnp.minimum(jnp.minimum(up, left), diag)
                    return (r, r)
                _, rest = lax.scan(col_step, first, (d_row[1:], prev_row[1:], prev_row[:-1]))
                row = jnp.concatenate([first[None], rest])
                return (row, row)
            _, rows = lax.scan(row_step, row0, D[1:])
            return jnp.concatenate([row0[None], rows], axis=0)

        def _backtrack(R, T1, T2):
            L = T1 + T2 - 1

            def step(carry, _):
                i, j, done = carry
                valid = jnp.logical_not(done)
                cd = jnp.where((i > 0) & (j > 0), R[jnp.maximum(i - 1, 0), jnp.maximum(j - 1, 0)], BIG)
                cu = jnp.where(i > 0, R[jnp.maximum(i - 1, 0), j], BIG)
                cl = jnp.where(j > 0, R[i, jnp.maximum(j - 1, 0)], BIG)
                choice = jnp.argmin(jnp.stack([cd, cu, cl]))
                ni = jnp.where(choice <= 1, i - 1, i)
                nj = jnp.where((choice == 0) | (choice == 2), j - 1, j)
                at_origin = (i == 0) & (j == 0)
                ni = jnp.where(at_origin, 0, ni)
                nj = jnp.where(at_origin, 0, nj)
                return ((ni, nj, done | at_origin), (i, j, valid))
            init = (jnp.int32(T1 - 1), jnp.int32(T2 - 1), jnp.bool_(False))
            _, (i_idx, j_idx, valid) = lax.scan(step, init, None, length=L)
            return (i_idx, j_idx, valid)

        def _align_one(small, large):
            T_small, d = small.shape
            T_large = large.shape[0]
            D = _pairwise_euclidean(small, large)
            R = _dtw_cost(D)
            i_idx, j_idx, valid = _backtrack(R, T_small, T_large)
            contrib = small[i_idx] * valid[:, None].astype(small.dtype)
            expanded = jnp.zeros((T_large, d), dtype=small.dtype).at[j_idx].add(contrib)
            return expanded
        return jax.vmap(_align_one)(teacher_features, student_features)

    def _L0_ffn_ref(inputs, gate_kernel, w0, w1, wo):
        import jax, jax.numpy as jnp
        import numpy as np
        NUM_EXPERTS = 64
        TOP_K = 2
        B, S, EMB, MLP = (4, 512, 256, 512)
        b, s, e = inputs.shape
        x = inputs.reshape(b * s, e)
        gate_logits = jnp.einsum('te,ex->tx', x, gate_kernel)
        weights, selected = jax.lax.top_k(gate_logits, TOP_K)
        weights = jax.nn.softmax(weights.astype(jnp.float32), axis=-1)
        flat_experts = selected.reshape(-1)
        sort_idx = jnp.argsort(flat_experts)
        token_idx = sort_idx // TOP_K
        sorted_x = jnp.take(x, token_idx, axis=0)
        group_sizes = jnp.bincount(flat_experts, length=NUM_EXPERTS).astype(jnp.int32)
        h0 = jax.lax.ragged_dot(sorted_x, w0, group_sizes)
        h1 = jax.lax.ragged_dot(sorted_x, w1, group_sizes)
        inter = jax.nn.silu(h0) * h1
        out_sorted = jax.lax.ragged_dot(inter, wo, group_sizes)
        unsorted = jnp.take(out_sorted, jnp.argsort(sort_idx), axis=0)
        per_tok = unsorted.reshape(b * s, TOP_K, e)
        out = jnp.einsum('BKE,BK->BE', per_tok.astype(jnp.float32), weights)
        return out.reshape(b, s, e)
    x = x + _L0_attn_ref(_layernorm(x, axis=-1), L0_attn_A_log, L0_attn_W_delta, L0_attn_W_dt, L0_attn_b_dt, L0_attn_W_B, L0_attn_W_C, L0_attn_D)
    x = x + _L0_xattn_ref(ctx_1024, _layernorm(x, axis=-1))
    x = x + _L0_ffn_ref(_layernorm(x, axis=-1), L0_ffn_gate_kernel, L0_ffn_w0, L0_ffn_w1, L0_ffn_wo)
    return x

_drawn_inputs = setup_inputs


def setup_inputs(seed=0):
    import zlib

    import numpy as np

    out = dict(_drawn_inputs(seed))
    spreads = {'L0_attn_D': (1.0, 0.2)}
    factors = {}
    for name, (base, spread) in spreads.items():
        noise = np.random.default_rng([zlib.crc32(name.encode()), seed]).standard_normal(out[name].shape)
        drawn = base * np.exp(spread * noise) if base else spread * noise
        out[name] = jnp.asarray(drawn.astype(out[name].dtype))
    for name, factor in factors.items():
        out[name] = (out[name] * factor).astype(out[name].dtype)
    return out
```

```python
from contextlib import ExitStack

import concourse.bass as bass
from concourse import mybir

ALU = mybir.AluOpType
ACT = mybir.ActivationFunctionType
AX_X = mybir.AxisListType.X
F32 = mybir.dt.float32
F16 = mybir.dt.float16
BF16 = mybir.dt.bfloat16
I32 = mybir.dt.int32
U32 = mybir.dt.uint32

P = 128
B, L, D = 16, 256, 256
N = 16
R = 64
E, F = 64, 512
DC = D // P
FC = F // P
TOK = B * L
TT = TOK // P
NP = B // 2
PT = 2 * L
PTT = PT // P
EPS = 1e-5
BIG = 1e30
SEG = 8
SW = L // SEG
LAG = 4
STEPS = L + LAG * (SEG - 1)
CODE_ROWS = [96, 96, 64, 28]
BLK = 8
BR = L // BLK
assert sum(CODE_ROWS) == STEPS and SEG * B == P and BLK * B == P
WRING = 4
MT = E + 2 * TOK // P


class Chip:
    pass


def run(K, *stages):
    for stage in stages:
        with ExitStack() as K.ctx:
            stage(K)


def settle(eng):
    eng.nop(nofuse=True)


def tile_stats(dve, nc, sem, count, tiles, stats, mv):
    settle(dve)
    for t, tile in enumerate(tiles):
        m = nc.vector.bn_stats(stats[:, t, :], tile)
    m.then_inc(sem, 1)
    dve.wait_ge(sem, count + 1)
    settle(dve)
    for t in range(len(tiles)):
        m = nc.vector.bn_aggr(mv[:, t, :], stats[:, t, :])
    m.then_inc(sem, 1)


def refined_scales(dve, nc, sem, count, mv, var, rstd, nmr):
    r, t = rstd[:, :], nmr[:, :]
    nc.vector.reciprocal(r, mv[:, :, 1]).then_inc(sem, 1)
    dve.wait_ge(sem, count + 1)
    nc.vector.tensor_tensor(t, r, r, ALU.mult).then_inc(sem, 1)
    dve.wait_ge(sem, count + 2)
    nc.vector.tensor_tensor(t, t, var[:, :], ALU.mult).then_inc(sem, 1)
    dve.wait_ge(sem, count + 3)
    nc.vector.tensor_scalar(t, t, -0.5, 1.5, ALU.mult, ALU.add).then_inc(sem, 1)
    dve.wait_ge(sem, count + 4)
    nc.vector.tensor_tensor(r, r, t, ALU.mult).then_inc(sem, 1)
    dve.wait_ge(sem, count + 5)
    nc.vector.scalar_tensor_tensor(out=t, in0=mv[:, :, 0], scalar=-1.0, in1=r, op0=ALU.mult,
                                   op1=ALU.mult).then_inc(sem, 1)


def load_and_constants(K):
    nc, sem = K.nc, K.sem
    w_in = sem("w_in")
    a_in = sem("a_in")
    a_exp = sem("a_exp")
    ident0 = sem("ident0")
    sel0 = sem("sel0")
    consts = sem("consts")
    x_in = [sem(f"x_in{g}") for g in range(NP)]
    st = sem("ln1_stats")
    root = sem("ln1_root")
    stats = K.ctx.enter_context(nc.sbuf_tensor("ln1_stats_sb", [P, TT, 6], F32))
    mv = K.ctx.enter_context(nc.sbuf_tensor("ln1_mv", [P, TT, 2], F32))
    var = K.ctx.enter_context(nc.sbuf_tensor("ln1_var", [P, TT], F32))

    block = K.ctx.enter_context(nc.Block())

    @block.sync
    def _(sp):
        for g in range(NP):
            sp.dma_start(K.x[:, g * PTT:(g + 1) * PTT, :],
                         K.x_dram[g * PT:(g + 1) * PT, :].rearrange("(t p) d -> p t d", p=P)).then_inc(x_in[g], 16)

    @block.scalar
    def _(act):
        act.dma_start(K.a_neg[:, :, :], K.a_log_dram.rearrange("(c p) n -> p c n", p=P)).then_inc(a_in, 16)
        act.dma_start(K.w_delta[:, :, :], K.w_delta_dram.rearrange("(c p) r -> p c r", p=P)).then_inc(w_in, 16)
        act.dma_start(K.w_dt[:, :], K.w_dt_dram).then_inc(w_in, 16)
        act.dma_start(K.b_dt[:, :], K.b_dt_dram.rearrange("(c p) -> p c", p=P),
                      allow_slow_non_contiguous=True).then_inc(w_in, 16)
        act.dma_start(K.d_skip[:, :], K.d_skip_dram.rearrange("(c p) -> p c", p=P),
                      allow_slow_non_contiguous=True).then_inc(w_in, 16)
        act.dma_start(K.w_bc[:, :, 0:N], K.w_b_dram.rearrange("(c p) n -> p c n", p=P)).then_inc(w_in, 16)
        act.dma_start(K.w_bc[:, :, N:2 * N], K.w_c_dram.rearrange("(c p) n -> p c n", p=P)).then_inc(w_in, 16)
        act.dma_start(K.gate[:, :, :], K.gate_dram.rearrange("(c p) e -> p c e", p=P)).then_inc(w_in, 16)
        act.wait_ge(a_in, 16)
        nc.scalar.activation(K.a_neg[:, :, :], K.a_neg[:, :, :], ACT.Exp).then_inc(a_exp, 1)
        act.wait_ge(w_in, 16 * 7)
        act.wait_ge(st, NP * 2 + 1)
        nc.scalar.activation(mv[:, :, 1], var[:, :], ACT.Sqrt).then_inc(root, 1)

    @block.vector
    def _(dve):
        for g in range(NP):
            dve.wait_ge(x_in[g], 16)
            tile_stats(dve, nc, st, g * 2, [K.x[:, g * PTT + t, :] for t in range(PTT)],
                       stats[:, g * PTT:(g + 1) * PTT, :], mv[:, g * PTT:(g + 1) * PTT, :])
        dve.wait_ge(st, NP * 2)
        nc.vector.tensor_scalar(var[:, :], mv[:, :, 1], EPS, None, ALU.add).then_inc(st, 1)
        dve.wait_ge(root, 1)
        refined_scales(dve, nc, st, NP * 2 + 1, mv, var, K.rstd, K.nmr)
        dve.wait_ge(a_exp, 1)
        nc.vector.tensor_scalar(K.a_neg[:, :, :], K.a_neg[:, :, :], -1.0, None, ALU.mult).then_inc(consts, 1)

    @block.gpsimd
    def _(pool):
        nc.gpsimd.memset(K.ident[:, :], 0.0).then_inc(ident0, 1)
        nc.gpsimd.memset(K.bc_sel[:, :, :], 0.0).then_inc(sel0, 1)
        pool.wait_ge(ident0, 1)
        nc.gpsimd.affine_select(out=K.ident[:, :], in_=K.ident[:, :], compare_op=ALU.not_equal, fill=1.0, base=0,
                                pattern=[[-1, P]], channel_multiplier=1).then_inc(consts, 1)
        for q in range(3):
            pool.wait_ge(sel0, q + 1)
            nc.gpsimd.affine_select(out=K.bc_sel[:, :, :], in_=K.bc_sel[:, :, :], compare_op=ALU.not_equal,
                                    fill=1.0, base=-2 * N * q, pattern=[[-1, 2 * N], [0, P]],
                                    channel_multiplier=1).then_inc(sel0, 1)


def prepare(K):
    nc, sem = K.nc, K.sem
    with ExitStack() as c:
        sb = lambda name, shape, dt=F32: c.enter_context(nc.sbuf_tensor(name, shape, dt))
        ps = lambda name, shape: c.enter_context(nc.psum_tensor(name, shape, F32))
        xn = [sb(f"pr_xn{u}", [P, PTT, D]) for u in range(2)]
        low = sb("pr_low", [R, PT])
        z_sb = sb("pr_z_sb", [P, DC, PT])
        az = sb("pr_az", [P, DC, PT])
        uz = az
        ez = sb("pr_ez", [P, DC, PT])
        lz = sb("pr_lz", [P, DC, PT])
        mz = sb("pr_mz", [P, DC, PT])
        cz = sb("pr_cz", [P, DC, PT])
        rest = sb("pr_rest", [2 * N, PT])
        mid = sb("pr_mid", [2 * N, PT], BF16)
        hi = sb("pr_hi", [2 * N, PT], BF16)
        xt_ps = [ps(f"pr_xt{u}", [P, DC, PT]) for u in range(2)]
        low_ps = ps("pr_low_ps", [P, PT])
        z_ps = ps("pr_z", [P, DC, PT])
        bc_ps = ps("pr_bc", [P, PT])

        norm = sem("pr_norm")
        turned = sem("pr_turned")
        xt_ok = sem("pr_xt_ok")
        low_mm, low_ok = sem("pr_low_mm"), sem("pr_low_ok")
        z_ok = sem("pr_z_ok")
        z_mm = sem("pr_z_mm")
        bc_mm = sem("pr_bc_mm")
        a_abs, a_exp, a_ln = sem("pr_abs"), sem("pr_exp"), sem("pr_ln")
        d_max, d_u, d_c = sem("pr_max"), sem("pr_u"), sem("pr_c")
        p_s, p_delta, p_dx = sem("pr_s"), sem("pr_delta"), sem("pr_dx")
        s_hi, s_rest, s_mid, s_lo, s_midc, s_hic = (sem("pr_" + x) for x in ("hi", "rst", "mid", "lo", "midc", "hic"))
        block = c.enter_context(nc.Block())

        @block.vector
        def _(dve):
            with dve.Fori(0, NP // 2) as q:
                for u in range(2):
                    p = q * 2 + u
                    dve.wait_ge(turned, p + 1)
                    nc.vector.tensor_copy(K.xt[:, :, bass.ds(p * PT, PT)], xt_ps[u][:, :, :]).then_inc(xt_ok, 1)
                    dve.wait_ge(bc_mm, p + 1)
                    dve.wait_ge(s_hi, p + 1)
                    dve.wait_ge(s_mid, p)
                    dve.wait_ge(s_lo, p)
                    nc.vector.tensor_tensor(rest[:, :], bc_ps[0:2 * N, :], hi[:, :], ALU.subtract).then_inc(s_rest, 1)
                    dve.wait_ge(z_ok, p + 1)
                    dve.wait_ge(p_delta, p)
                    nc.vector.tensor_scalar(mz[:, :, :], z_sb[:, :, :], 0.0, None, ALU.max).then_inc(d_max, 1)
                    dve.wait_ge(s_mid, p + 1)
                    nc.vector.tensor_tensor(K.bc3[4 * N:6 * N, bass.ds(p * PT, PT)], rest[:, :], mid[:, :],
                                            ALU.subtract).then_inc(s_lo, 1)
                    dve.wait_ge(a_exp, p + 1)
                    nc.vector.tensor_scalar(uz[:, :, :], ez[:, :, :], 1.0, None, ALU.add).then_inc(d_u, 1)
                    dve.wait_ge(d_u, p + 1)
                    dve.wait_ge(p_s, p)
                    nc.vector.scalar_tensor_tensor(out=cz[:, :, :], in0=uz[:, :, :], scalar=-1.0, in1=ez[:, :, :],
                                                   op0=ALU.add, op1=ALU.subtract).then_inc(d_c, 1)

        @block.scalar
        def _(act):
            with act.Fori(0, NP // 2) as q:
                for u in range(2):
                    p = q * 2 + u
                    act.wait_ge(turned, p if u == 0 else p - 1)
                    for t in range(PTT):
                        nc.scalar.activation(xn[u][:, t, :],
                                             K.x[:, bass.ds(p * PTT + t, 1), :].rearrange("p a d -> p (a d)"),
                                             ACT.Identity, bias=K.nmr[:, bass.ds(p * PTT + t, 1)],
                                             scale=K.rstd[:, bass.ds(p * PTT + t, 1)]).then_inc(norm, 1)
                    act.wait_ge(low_mm, p + 1)
                    act.wait_ge(z_mm, p)
                    nc.scalar.activation(low[:, :], low_ps[0:R, :], ACT.Copy).then_inc(low_ok, 1)
                    act.wait_ge(bc_mm, p + 1)
                    act.wait_ge(s_rest, p)
                    act.wait_ge(s_hic, p)
                    nc.scalar.activation(hi[:, :], bc_ps[0:2 * N, :], ACT.Copy).then_inc(s_hi, 1)
                    act.wait_ge(s_hi, p + 1)
                    nc.scalar.activation(K.bc3[0:2 * N, bass.ds(p * PT, PT)], hi[:, :], ACT.Copy).then_inc(s_hic, 1)
                    act.wait_ge(s_rest, p + 1)
                    act.wait_ge(s_midc, p)
                    act.wait_ge(s_lo, p)
                    nc.scalar.activation(mid[:, :], rest[:, :], ACT.Copy).then_inc(s_mid, 1)
                    act.wait_ge(s_mid, p + 1)
                    nc.scalar.activation(K.bc3[2 * N:4 * N, bass.ds(p * PT, PT)], mid[:, :], ACT.Copy).then_inc(s_midc, 1)
                    act.wait_ge(z_mm, p + 1)
                    act.wait_ge(d_max, p)
                    for c_ in range(DC):
                        m = nc.scalar.activation(z_sb[:, c_, :], z_ps[:, c_, :], ACT.Identity,
                                                 bias=K.b_dt[:, c_:c_ + 1])
                    m.then_inc(z_ok, 1)
                    act.wait_ge(z_ok, p + 1)
                    act.wait_ge(d_c, p)
                    nc.scalar.activation(az[:, :, :], z_sb[:, :, :], ACT.Abs).then_inc(a_abs, 1)
                    act.wait_ge(a_abs, p + 1)
                    nc.scalar.activation(ez[:, :, :], az[:, :, :], ACT.Exp, scale=-1.0).then_inc(a_exp, 1)
                    act.wait_ge(a_exp, p + 1)
                    act.wait_ge(p_s, p)
                    nc.scalar.activation(lz[:, :, :], ez[:, :, :], ACT.Ln, bias=1.0).then_inc(a_ln, 1)

        @block.gpsimd
        def _(pool):
            with pool.Fori(0, NP // 2) as q:
                for u in range(2):
                    p = q * 2 + u
                    cols = bass.ds(p * PT, PT)
                    pool.wait_ge(a_ln, p + 1)
                    pool.wait_ge(d_c, p + 1)
                    nc.gpsimd.tensor_tensor(K.delta[:, :, cols], lz[:, :, :], cz[:, :, :], ALU.subtract).then_inc(p_s, 1)
                    pool.wait_ge(p_s, p + 1)
                    pool.wait_ge(d_max, p + 1)
                    settle(pool)
                    nc.gpsimd.tensor_tensor(K.delta[:, :, cols], K.delta[:, :, cols], mz[:, :, :],
                                            ALU.add).then_inc(p_delta, 1)
                    pool.wait_ge(p_delta, p + 1)
                    pool.wait_ge(xt_ok, p + 1)
                    nc.gpsimd.tensor_tensor(K.dx[:, :, cols], K.delta[:, :, cols], K.xt[:, :, cols],
                                            ALU.mult).then_inc(p_dx, 1)

        @block.tensor
        def _(pe):
            with pe.Fori(0, NP // 2) as q:
                for u in range(2):
                    p = q * 2 + u
                    cols = bass.ds(p * PT, PT)
                    pe.wait_ge(norm, (p + 1) * PTT)
                    pe.wait_ge(xt_ok, p if u == 0 else p - 1)
                    for c_ in range(DC):
                        for t in range(PTT):
                            m = nc.tensor.transpose(xt_ps[u][:, c_, t * P:(t + 1) * P],
                                                    xn[u][:, t, c_ * P:(c_ + 1) * P], K.ident[:, :])
                    m.then_inc(turned, 1)
                    pe.wait_ge(xt_ok, p + 1)
                    pe.wait_ge(low_ok, p)
                    pe.wait_ge(s_rest, p)
                    for c_ in range(DC):
                        m = nc.tensor.matmul(low_ps[0:R, :], K.w_delta[:, c_, :], K.xt[:, c_, cols],
                                             start=(c_ == 0), stop=(c_ == DC - 1))
                    m.then_inc(low_mm, 1)
                    for c_ in range(DC):
                        m = nc.tensor.matmul(bc_ps[0:2 * N, :], K.w_bc[:, c_, :], K.xt[:, c_, cols],
                                             start=(c_ == 0), stop=(c_ == DC - 1))
                    m.then_inc(bc_mm, 1)
                    pe.wait_ge(low_ok, p + 1)
                    pe.wait_ge(z_ok, p)
                    for c_ in range(DC):
                        m = nc.tensor.matmul(z_ps[:, c_, :], K.w_dt[:, c_ * P:(c_ + 1) * P], low[:, :],
                                             start=True, stop=True)
                    m.then_inc(z_mm, 1)


def scan_states(K):
    nc, sem = K.nc, K.sem
    S = N * DC
    RING = 4
    with ExitStack() as c:
        sb = lambda name, shape, dt=F32: c.enter_context(nc.sbuf_tensor(name, shape, dt))
        ps = lambda name, shape: c.enter_context(nc.psum_tensor(name, shape, F32))
        b_sb = [sb(f"sc_b{i}", [P, PT]) for i in range(2)]
        u_sb = [sb(f"sc_u{i}", [P, PT]) for i in range(RING)]
        h_sb = [sb(f"sc_h{i}", [P, PT]) for i in range(RING)]
        hc_sb = [sb(f"sc_hc{i}", [P, PT]) for i in range(RING)]
        y_ps = ps("sc_y", [P, DC, PT])
        da_ps = [ps(f"sc_da{i}", [P, PT]) for i in range(2)]
        b_ps = [ps(f"sc_bps{i}", [P, PT]) for i in range(2)]
        c_ps = [ps(f"sc_cps{i}", [P, PT]) for i in range(2)]
        da0 = sem("sc_da0")
        spread = sem("sc_spread")
        spread_cs = sem("sc_spread_cs")
        da_ok = sem("sc_da_ok")
        y_out = sem("sc_y_out")
        b_ok = sem("sc_b_ok")
        u_ok = sem("sc_u_ok")
        h_ok = sem("sc_h_ok")
        hc_ok = sem("sc_hc_ok")
        summed = sem("sc_summed")
        block = c.enter_context(nc.Block())

        def done(p, s, ago=0, unit=S):
            return p * unit + (RING + s - ago + 1)

        @block.scalar
        def _(act):
            act.sem_inc(b_ok, RING)
            act.wait_ge(da0, 2)

            def copy_b(p, n):
                act.wait_ge(spread, p * N + n + 1)
                act.wait_ge(u_ok, done(p, n * DC + 1, 2 * DC))
                nc.scalar.activation(b_sb[n % 2][:, :], b_ps[n % 2][:, :], ACT.Copy).then_inc(b_ok, 1)

            def pair(p, last):
                for n in range(N):
                    if not last or n + 1 < N:
                        copy_b(p, n + 1)
                    for dh in range(DC):
                        s = n * DC + dh
                        act.wait_ge(h_ok, done(p, s, 2))
                        settle(act)
                        cols = bass.ds(p * PT, PT)
                        o = da_ps[dh][:, :].rearrange("p (b l) -> p b l", b=2)[:, :, 1:L]
                        i = K.delta[:, dh, cols].rearrange("p (b l) -> p b l", b=2)[:, :, 1:L]
                        nc.scalar.activation(o, i, ACT.Exp, scale=K.a_neg[:, dh, n:n + 1]).then_inc(da_ok, 1)

            copy_b(0, 0)
            with act.Fori(0, NP - 1) as p:
                pair(p, False)
            pair(NP - 1, True)

        @block.gpsimd
        def _(pool):
            pool.sem_inc(u_ok, RING)
            with pool.Fori(0, NP) as p:
                for n in range(N):
                    for dh in range(DC):
                        s = n * DC + dh
                        pool.wait_ge(b_ok, done(p, n, unit=N))
                        pool.wait_ge(h_ok, done(p, s, RING))
                        settle(pool)
                        nc.gpsimd.tensor_tensor(u_sb[s % RING][:, :], K.dx[:, dh, bass.ds(p * PT, PT)],
                                                b_sb[n % 2][:, :], ALU.mult).then_inc(u_ok, 1)

        @block.vector
        def _(dve):
            for i in range(2):
                nc.vector.memset(da_ps[i][:, :], 0.0).then_inc(da0, 1)
            dve.sem_inc(h_ok, RING)
            dve.sem_inc(hc_ok, RING)

            def scan(p, s):
                dve.wait_ge(da_ok, p * S + s + 1)
                dve.wait_ge(u_ok, done(p, s))
                dve.wait_ge(hc_ok, done(p, s, RING))
                nc.vector.tensor_tensor_scan(h_sb[s % RING][:, :], da_ps[s % 2][:, :], u_sb[s % RING][:, :], 0.0,
                                             ALU.mult, ALU.add).then_inc(h_ok, 1)

            def times_c(p, s):
                dve.wait_ge(h_ok, done(p, s))
                dve.wait_ge(summed, done(p, s, RING))
                dve.wait_ge(spread_cs, p * N + s // DC + 1)
                nc.vector.tensor_tensor(hc_sb[s % RING][:, :], h_sb[s % RING][:, :], c_ps[(s // DC) % 2][:, :],
                                        ALU.mult).then_inc(hc_ok, 1)

            def pair(p, last):
                for n in range(N):
                    if n + 1 < N:
                        for dh in range(DC):
                            scan(p, (n + 1) * DC + dh)
                    for dh in range(DC):
                        times_c(p, n * DC + dh)
                if not last:
                    for dh in range(DC):
                        scan(p + 1, dh)
                dve.wait_ge(summed, done(p, S - 1))
                for dh in range(DC):
                    cols = bass.ds(p * PT, PT)
                    nc.vector.scalar_tensor_tensor(out=K.delta[:, dh, cols], in0=K.xt[:, dh, cols],
                                                   scalar=K.d_skip[:, dh:dh + 1], in1=y_ps[:, dh, :],
                                                   op0=ALU.mult, op1=ALU.add).then_inc(y_out, 1)

            for dh in range(DC):
                scan(0, dh)
            with dve.Fori(0, NP - 1) as p:
                pair(p, False)
            pair(NP - 1, True)

        @block.tensor
        def _(pe):
            pe.sem_inc(summed, RING)

            def spread_b(p, n):
                pe.wait_ge(b_ok, done(p, n, 2, N))
                nc.tensor.matmul(b_ps[n % 2][:, :], K.bc_sel[:, n % N, :], K.bc3[:, bass.ds((p + n // N) * PT, PT)],
                                 start=True, stop=True).then_inc(spread, 1)

            def spread_c(p, n):
                nc.tensor.matmul(c_ps[n % 2][:, :], K.bc_sel[:, N + n % N, :],
                                 K.bc3[:, bass.ds((p + n // N) * PT, PT)], start=True,
                                 stop=True).then_inc(spread_cs, 1)

            def pair(p, last):
                for n in range(N):
                    if not last or n + 3 < N:
                        spread_b(p, n + 3)
                    pe.wait_ge(hc_ok, done(p, n * DC + 1))
                    if not last or n + 2 < N:
                        spread_c(p, n + 2)
                    if n == 0:
                        pe.wait_ge(y_out, p * DC)
                    for dh in range(DC):
                        s = n * DC + dh
                        nc.tensor.matmul(y_ps[:, dh, :], K.ident[:, :], hc_sb[s % RING][:, :], start=(n == 0),
                                         stop=(n == N - 1)).then_inc(summed, 1)

            for n in range(2):
                spread_b(0, n)
                spread_c(0, n)
            spread_b(0, 2)
            with pe.Fori(0, NP - 1) as p:
                pair(p, False)
            pair(NP - 1, True)


def distances(K):
    nc, sem = K.nc, K.sem
    with ExitStack() as c:
        sb = lambda name, shape, dt=F32: c.enter_context(nc.sbuf_tensor(name, shape, dt))
        ps = lambda name, shape: c.enter_context(nc.psum_tensor(name, shape, F32))
        old = K.xt[:, :, :].rearrange("p c t -> p (c t)")
        slot = lambda i: old[:, i * PTT * D:(i + 1) * PTT * D]
        cx = [slot(u).rearrange("p (t d) -> p t d", t=PTT) for u in range(2)]
        yt = [slot(2 + u).rearrange("p (c t) -> p c t", c=DC) for u in range(2)]
        s_sb = [slot(4 + u).rearrange("p (t d) -> p t d", t=PTT) for u in range(2)]
        st_sb = [slot(6 + u).rearrange("p (c t) -> p c t", c=DC) for u in range(2)]
        sq = [sb(f"di_sq{u}", [P, DC, PT]) for u in range(2)]
        ct_sb = [sb(f"di_ct{u}", [P, DC, PT]) for u in range(2)]
        dd = [sb(f"di_dd{u}", [P, PTT, L]) for u in range(2)]
        aa = [sb(f"di_aa{u}", [P, PTT]) for u in range(2)]
        junk = [sb(f"di_junk{u}", [P, PTT, D]) for u in range(2)]
        ones = sb("di_ones", [P, P])
        stats = sb("di_stats", [P, PTT, 6])
        mv = sb("di_mv", [P, PTT, 2])
        var = sb("di_var", [P, PTT])
        rstd = [sb(f"di_rstd{u}", [P, PTT]) for u in range(2)]
        nmr = [sb(f"di_nmr{u}", [P, PTT]) for u in range(2)]
        y_ps = ps("di_y", [P, PTT, D])
        st_ps = ps("di_st_ps", [P, DC, PT])
        ct_ps = ps("di_ct_ps", [P, DC, PT])
        d_ps = ps("di_d_ps", [P, PTT, L])

        set_up = sem("di_set_up")
        ctx_in = [sem(f"di_ctx_in{u}") for u in range(2)]
        yt_ok = sem("di_yt_ok")
        y_tr = sem("di_y_tr")
        x_ok = sem("di_x_ok")
        stt = sem("di_stats_ok")
        root = sem("di_root")
        s_ok = sem("di_s_ok")
        st_tr, st_ok, sq_ok = sem("di_st_tr"), sem("di_st_ok"), sem("di_sq_ok")
        ct_tr, ct_ok, aa_ok = sem("di_ct_tr"), sem("di_ct_ok"), sem("di_aa_ok")
        d_mm, d_ok = sem("di_d_mm"), sem("di_d_ok")
        stored = [sem(f"di_stored{u}") for u in range(2)]
        K.wave_in = sem("wave_in")
        SS = 9
        block = c.enter_context(nc.Block())
        x_rows = lambda p: K.x[:, bass.ds(p * PTT, PTT), :]

        @block.sync
        def _(sp):
            def load_ctx(p):
                if p >= 2:
                    sp.wait_ge(ct_tr, p - 1)
                    sp.wait_ge(aa_ok, p - 1)
                sp.dma_start(cx[p % 2], K.ctx_dram[2 * p:2 * p + 2, :, :].rearrange("b (h p) d -> p (b h) d", p=P)
                             ).then_inc(ctx_in[p % 2], 16)

            load_ctx(0)
            load_ctx(1)
            sp.wait_ge(set_up, 2)
            for p in range(NP):
                if p >= 1 and p + 1 < NP:
                    load_ctx(p + 1)
                sp.wait_ge(stored[p % 2], p // 2 * 16 + 16)
                for s in range(SEG):
                    sp.dma_start(K.wave[s * B + 2 * p:s * B + 2 * p + 2, s * LAG * SW:(s * LAG + L) * SW].rearrange(
                                     "b (i j) -> b i j", j=SW),
                                 K.dist_dram[2 * p:2 * p + 2, :, s * SW:(s + 1) * SW]).then_inc(K.wave_in, 16)
            sp.wait_ge(K.wave_in, 16 * SEG * NP)

        @block.gpsimd
        def _(pool):
            nc.gpsimd.memset(ones[:, :], 1.0).then_inc(set_up, 1)
            nc.gpsimd.memset(K.wave[:, :], 0.0).then_inc(set_up, 1)
            with pool.Fori(0, NP // 2) as q:
                for u in range(2):
                    p = q * 2 + u
                    pool.wait_ge(y_tr, p if u == 0 else p - 1)
                    nc.gpsimd.tensor_copy(yt[u], K.delta[:, :, bass.ds(p * PT, PT)]).then_inc(yt_ok, 1)

        @block.vector
        def _(dve):
            with dve.Fori(0, NP // 2) as q:
                for u in range(2):
                    p = q * 2 + u
                    dve.wait_ge(y_tr, p + 1)
                    nc.vector.tensor_tensor(x_rows(p), x_rows(p), y_ps[:, :, :], ALU.add).then_inc(x_ok, 1)
                    dve.wait_ge(x_ok, p + 1)
                    tile_stats(dve, nc, stt, p * SS, [K.x[:, bass.ds(p * PTT + t, 1), :].rearrange("p a d -> p (a d)")
                                                      for t in range(PTT)], stats, mv)
                    dve.wait_ge(stt, p * SS + 2)
                    nc.vector.tensor_scalar(var[:, :], mv[:, :, 1], EPS, None, ALU.add).then_inc(stt, 1)
                    dve.wait_ge(ct_tr, p + 1)
                    dve.wait_ge(d_mm, p if u == 0 else p - 1)
                    nc.vector.tensor_scalar(ct_sb[u][:, :, :], ct_ps[:, :, :], -2.0, None, ALU.mult).then_inc(ct_ok, 1)
                    dve.wait_ge(root, p + 1)
                    dve.wait_ge(s_ok, p if u == 0 else p - 1)
                    refined_scales(dve, nc, stt, p * SS + 3, mv, var, rstd[u], nmr[u])

        @block.scalar
        def _(act):
            with act.Fori(0, NP // 2) as q:
                for u in range(2):
                    p = q * 2 + u
                    act.wait_ge(ctx_in[u], q * 16 + 16)
                    act.wait_ge(d_ok, p if u == 0 else p - 1)
                    for t in range(PTT):
                        m = nc.scalar.activation(junk[u][:, t, :], cx[u][:, t, :], ACT.Square, accum_out=aa[u][:, t:t + 1])
                    m.then_inc(aa_ok, 1)
                    act.wait_ge(stt, p * SS + 3)
                    nc.scalar.activation(mv[:, :, 1], var[:, :], ACT.Sqrt).then_inc(root, 1)
                    act.wait_ge(stt, p * SS + SS)
                    act.wait_ge(st_tr, p if u == 0 else p - 1)
                    for t in range(PTT):
                        m = nc.scalar.activation(s_sb[u][:, t, :],
                                                 K.x[:, bass.ds(p * PTT + t, 1), :].rearrange("p a d -> p (a d)"),
                                                 ACT.Identity, bias=nmr[u][:, t:t + 1], scale=rstd[u][:, t:t + 1])
                    m.then_inc(s_ok, 1)
                    act.wait_ge(st_tr, p + 1)
                    act.wait_ge(d_mm, p if u == 0 else p - 1)
                    nc.scalar.activation(st_sb[u], st_ps[:, :, :], ACT.Copy).then_inc(st_ok, 1)
                    act.wait_ge(st_ok, p + 1)
                    nc.scalar.activation(sq[u][:, :, :], st_sb[u], ACT.Square).then_inc(sq_ok, 1)
                    act.wait_ge(d_mm, p + 1)
                    act.wait_ge(stored[u], q * 16)
                    for t in range(PTT):
                        m = nc.scalar.activation(dd[u][:, t, :], d_ps[:, t, :], ACT.Relu, bias=aa[u][:, t:t + 1])
                    m.then_inc(d_ok, 1)
                    act.wait_ge(d_ok, p + 1)
                    act.dma_start(K.dist_dram[bass.ds(p * 2, 2), :, :].rearrange("b (h p) d -> p (b h) d", p=P),
                                  dd[u][:, :, :]).then_inc(stored[u], 16)

        @block.tensor
        def _(pe):
            pe.wait_ge(set_up, 1)
            with pe.Fori(0, NP // 2) as q:
                for u in range(2):
                    p = q * 2 + u
                    pe.wait_ge(yt_ok, p + 1)
                    pe.wait_ge(x_ok, p)
                    for t in range(PTT):
                        for c_ in range(DC):
                            m = nc.tensor.transpose(y_ps[:, t, c_ * P:(c_ + 1) * P], yt[u][:, c_, t * P:(t + 1) * P],
                                                    K.ident[:, :])
                    m.then_inc(y_tr, 1)
                    pe.wait_ge(ctx_in[u], q * 16 + 16)
                    pe.wait_ge(ct_ok, p)
                    for t in range(PTT):
                        for c_ in range(DC):
                            m = nc.tensor.transpose(ct_ps[:, c_, t * P:(t + 1) * P], cx[u][:, t, c_ * P:(c_ + 1) * P],
                                                    K.ident[:, :])
                    m.then_inc(ct_tr, 1)
                    pe.wait_ge(s_ok, p + 1)
                    pe.wait_ge(st_ok, p)
                    for t in range(PTT):
                        for c_ in range(DC):
                            m = nc.tensor.transpose(st_ps[:, c_, t * P:(t + 1) * P], s_sb[u][:, t, c_ * P:(c_ + 1) * P],
                                                    K.ident[:, :])
                    m.then_inc(st_tr, 1)
                    pe.wait_ge(sq_ok, p + 1)
                    pe.wait_ge(ct_ok, p + 1)
                    pe.wait_ge(d_ok, p)
                    for t in range(PTT):
                        j = slice(t // 2 * L, (t // 2 + 1) * L)
                        for c_ in range(DC):
                            nc.tensor.matmul(d_ps[:, t, :], ct_sb[u][:, c_, t * P:(t + 1) * P], st_sb[u][:, c_, j],
                                             start=(c_ == 0), stop=False)
                        for c_ in range(DC):
                            m = nc.tensor.matmul(d_ps[:, t, :], ones[:, :], sq[u][:, c_, j], start=False,
                                                 stop=(c_ == DC - 1))
                    m.then_inc(d_mm, 1)


def wave(K):
    nc, sem = K.nc, K.sem
    with ExitStack() as c:
        sb = lambda name, shape, dt=F32: c.enter_context(nc.sbuf_tensor(name, shape, dt))
        r = sb("wv_r", [P, STEPS + 1 + LAG, SW + 1])
        m_sb = [sb(f"wv_m{i}", [P, SW]) for i in range(2)]
        zeros = sb("wv_zeros", [P, E // 8 * D])
        least = sb("wv_least", [P, CODE_ROWS[0] * SW])
        code = sb("wv_code", [P, STEPS, 2, SW], F16)
        shift = sb("wv_shift", [P, P])
        edge_big = sb("wv_edge_big", [P, 1])
        first = sb("wv_first", [P, 1])
        e_ps = [c.enter_context(nc.psum_tensor(f"wv_e{i}", [P, 512], F32)) for i in range(4)]
        set_up = sem("wv_set_up")
        mats = sem("wv_mats")
        roots = sem("wv_roots")
        m_ok = sem("wv_m_ok")
        r_ok = sem("wv_r_ok")
        e_mm = sem("wv_e_mm")
        edge_ok = sem("wv_edge_ok")
        least_ok, code_ok = sem("wv_least_ok"), sem("wv_code_ok")
        K.code_in = sem("code_in")
        zeros_ok, zeros_out = sem("wv_zeros_ok"), sem("wv_zeros_out")
        G = 4
        block = c.enter_context(nc.Block())

        @block.gpsimd
        def _(pool):
            nc.gpsimd.memset(zeros[:, :], 0.0).then_inc(zeros_ok, 1)
            nc.gpsimd.memset(shift[:, :], 0.0).then_inc(mats, 1)
            nc.gpsimd.memset(edge_big[:, :], 0.0).then_inc(mats, 1)
            nc.gpsimd.memset(first[:, :], BIG).then_inc(mats, 1)
            pool.wait_ge(mats, 3)
            nc.gpsimd.affine_select(out=shift[:, :], in_=shift[:, :], compare_op=ALU.not_equal, fill=1.0, base=B,
                                    pattern=[[-1, P]], channel_multiplier=1).then_inc(set_up, 1)
            nc.gpsimd.memset(edge_big[0:B, :], BIG).then_inc(set_up, 1)
            nc.gpsimd.memset(first[0:B, :], 0.0).then_inc(set_up, 1)

        @block.sync
        def _(sp):
            sp.wait_ge(zeros_ok, 1)
            rest = (MT - E) // 8
            for k in range(8):
                rows = (E + k * rest) * P
                sp.dma_start(K.outs_dram[rows:rows + rest * P, :].rearrange("(p t) d -> p (t d)", p=P),
                             zeros[:, 0:rest * D]).then_inc(zeros_out, 16)
            done, n = 0, 0
            for k in range(BLK):
                for s in range(SEG):
                    t0 = k * BR + s * LAG
                    while done < t0 + BR:
                        done += CODE_ROWS[n]
                        n += 1
                        sp.wait_ge(code_ok, 2 * n)
                    sp.dma_start(K.codes[k * B:(k + 1) * B, s, :, :, :].rearrange("p i a j -> p (i a j)"),
                                 code[s * B:(s + 1) * B, t0:t0 + BR, :, :].rearrange("p i a j -> p (i a j)")
                                 ).then_inc(K.code_in, 16)
            sp.wait_ge(K.code_in, 16 * BLK * SEG)
            sp.wait_ge(zeros_out, 16 * 8)

        @block.vector
        def _(dve):
            nc.vector.memset(r[:, 0, :], BIG).then_inc(m_ok, 1)
            nc.vector.memset(r[:, 1:LAG + 1, 0:1], BIG).then_inc(edge_ok, LAG)
            dve.wait_ge(set_up, 3)

            def step(t, g):
                i = g % 2
                w = K.wave[:, bass.ds(t * SW, SW)]
                up = r[:, bass.ds(t, 1), :].rearrange("p a j -> p (a j)")
                row = r[:, bass.ds(t + 1, 1), :].rearrange("p a j -> p (a j)")
                if not (isinstance(t, int) and t == 0):
                    dve.wait_ge(r_ok, t)
                else:
                    dve.wait_ge(m_ok, 1)
                nc.vector.tensor_tensor(m_sb[i][:, :], up[:, 0:SW], up[:, 1:SW + 1], ALU.min).then_inc(m_ok, 1)
                dve.wait_ge(edge_ok, t + 1)
                dve.wait_ge(m_ok, t + 2)
                start = row[:, 0:1] if not (isinstance(t, int) and t == 0) else first[:, :]
                nc.vector.tensor_tensor_scan(row[:, 1:SW + 1], m_sb[i][:, :], w, start, ALU.min,
                                             ALU.add).then_inc(r_ok, 1)

            dve.wait_ge(roots, 1)
            for g in range(G):
                step(g, g)
            with dve.Fori(1, STEPS // G) as q:
                for g in range(G):
                    step(q * G + g, g)
            t = 0
            for n, rows in enumerate(CODE_ROWS):
                dve.wait_ge(r_ok, t + rows)
                dve.wait_ge(edge_ok, t + rows)
                left = r[:, t + 1:t + 1 + rows, 0:SW]
                up = r[:, t:t + rows, 1:SW + 1]
                diag = r[:, t:t + rows, 0:SW]
                ls = least[:, 0:rows * SW].rearrange("p (t j) -> p t j", j=SW)
                if n:
                    dve.wait_ge(code_ok, 2 * n)
                nc.vector.tensor_tensor(ls, up, diag, ALU.min).then_inc(least_ok, 1)
                nc.vector.tensor_tensor(code[:, t:t + rows, 1, :], up, diag, ALU.is_lt).then_inc(code_ok, 1)
                dve.wait_ge(least_ok, n + 1)
                nc.vector.tensor_tensor(code[:, t:t + rows, 0, :], left, ls, ALU.is_lt).then_inc(code_ok, 1)
                t += rows


        @block.scalar
        def _(act):
            nc.scalar.activation(K.wave[:, :], K.wave[:, :], ACT.Sqrt).then_inc(roots, 1)
            act.wait_ge(set_up, 3)
            with act.Fori(0, STEPS // G) as q:
                for g in range(G):
                    t = q * G + g
                    act.wait_ge(e_mm, t + 1)
                    settle(act)
                    nc.scalar.activation(r[:, bass.ds(t + LAG + 1, 1), 0:1].rearrange("p a j -> p (a j)"),
                                         e_ps[g][:, 0:1], ACT.Identity, bias=edge_big[:, :]).then_inc(edge_ok, 1)

        @block.tensor
        def _(pe):
            pe.wait_ge(set_up, 3)
            with pe.Fori(0, STEPS // G) as q:
                for g in range(G):
                    t = q * G + g
                    pe.wait_ge(edge_ok, q * G + g + 1)
                    pe.wait_ge(r_ok, t + 1)
                    nc.tensor.matmul(e_ps[g][:, 0:1], shift[:, :],
                                     r[:, bass.ds(t + 1, 1), SW:SW + 1].rearrange("p a j -> p (a j)"),
                                     start=True, stop=True).then_inc(e_mm, 1)


def trace_back(K):
    nc, sem = K.nc, K.sem
    MARK = 600.0
    with ExitStack() as c:
        sb = lambda name, shape, dt=F32: c.enter_context(nc.sbuf_tensor(name, shape, dt))
        left = sb("tb_left", [P, BR, L], F16)
        up = sb("tb_up", [P, BR, L], F16)
        dg = sb("tb_dg", [P, BR, L], F16)
        t1 = sb("tb_t1", [P, BR, L], F16)
        exits = sb("tb_exits", [P, BR, L], F16)
        col = sb("tb_col", [P, L], F16)
        col_m = sb("tb_col_m", [P, L], F16)
        maps = [sb(f"tb_map{i}", [P, 2 + L], F16) for i in range(2)]
        cand = [sb(f"tb_cand{i}", [P, L], F16) for i in range(3)]
        junk = [sb(f"tb_junk{i}", [P, L], F16) for i in range(2)]
        entry0 = sb("tb_entry0", [P, 1])
        entry = sb("tb_entry", [P, 1])
        found = sb("tb_found", [P, 1])
        hi = sb("tb_hi", [P, 1 + BR])
        ex = sb("tb_ex", [P, BR])
        off = sb("tb_off", [P, BR])
        lo = sb("tb_lo", [P, BR])
        shift = sb("tb_shift", [P, P])
        s_ps = c.enter_context(nc.psum_tensor("tb_s", [P, 512], F32))
        hi_ps = c.enter_context(nc.psum_tensor("tb_hi_ps", [P, 512], F32))
        lo_ps = c.enter_context(nc.psum_tensor("tb_lo_ps", [P, 512], F32))
        raw, set_up = sem("tb_raw"), sem("tb_set_up")
        cx_in = sem("tb_cx_in")
        st = sem("tb_steps")
        gathered = sem("tb_gathered")
        shifted = sem("tb_shifted")
        turned = sem("tb_turned")
        spread = sem("tb_spread")
        block = c.enter_context(nc.Block())

        @block.sync
        def _(sp):
            sp.wait_ge(st, 2)
            for p in range(NP):
                sp.dma_start(K.cx[:, p * PTT:(p + 1) * PTT, :],
                             K.ctx_dram[2 * p:2 * p + 2, :, :].rearrange("b (h p) d -> p (b h) d", p=P)
                             ).then_inc(cx_in, 16)
            sp.wait_ge(cx_in, 16 * NP)

        @block.gpsimd
        def _(pool):
            nc.gpsimd.memset(shift[:, :], 0.0).then_inc(raw, 1)
            nc.gpsimd.memset(entry0[:, :], float(L - 1)).then_inc(raw, 1)
            pool.wait_ge(raw, 2)
            nc.gpsimd.affine_select(out=shift[:, :], in_=shift[:, :], compare_op=ALU.not_equal, fill=1.0, base=-B,
                                    pattern=[[-1, P]], channel_multiplier=1).then_inc(set_up, 1)
            nc.gpsimd.affine_select(out=entry0[:, :], in_=entry0[:, :], compare_op=ALU.is_ge, fill=0.0,
                                    base=-B * (BLK - 1), pattern=[[0, 1]], channel_multiplier=1).then_inc(set_up, 1)
            nc.gpsimd.iota(col[:, :], [[1, L]], base=0, channel_multiplier=0,
                           allow_small_or_imprecise_dtypes=True).then_inc(set_up, 1)
            nc.gpsimd.iota(col_m[:, :], [[1, L]], base=int(MARK), channel_multiplier=0,
                           allow_small_or_imprecise_dtypes=True).then_inc(set_up, 1)
            nc.gpsimd.iota(maps[1][:, :], [[1, L + 2]], base=-2, channel_multiplier=0,
                           allow_small_or_imprecise_dtypes=True).then_inc(set_up, 1)
            nc.gpsimd.memset(maps[0][:, 0:2], 0.0).then_inc(set_up, 1)

        @block.vector
        def _(dve):
            n = [0]

            def did(ins):
                n[0] += 1
                ins.then_inc(st, 1)
                return n[0]

            view = lambda a: K.codes[:, :, :, a, :].rearrange("p s i j -> p i s j")
            to = lambda x: x[:, :, :].rearrange("p i (s j) -> p i s j", j=SW)
            dve.wait_ge(set_up, 6)
            a = did(nc.vector.tensor_copy(to(left), view(0)))
            did(nc.vector.tensor_tensor(to(up), view(1), view(0), ALU.is_gt))
            dve.wait_ge(st, n[0])
            did(nc.vector.tensor_tensor(t1[:, :, :], left[:, :, :], up[:, :, :], ALU.add))
            dve.wait_ge(st, n[0])
            did(nc.vector.tensor_scalar(dg[:, :, :], t1[:, :, :], -1.0, 1.0, ALU.mult, ALU.add))
            dve.wait_ge(st, n[0])

            bc = lambda x: x[:, :].rearrange("p (a j) -> p a j", a=1).broadcast_to([P, BR, L])
            did(nc.vector.tensor_tensor(t1[:, :, :], up[:, :, :], bc(col), ALU.mult))
            did(nc.vector.tensor_tensor(exits[:, :, :], dg[:, :, :], bc(col_m), ALU.mult))
            dve.wait_ge(st, n[0])
            did(nc.vector.tensor_tensor(t1[:, :, :], t1[:, :, :], exits[:, :, :], ALU.add))
            dve.wait_ge(st, n[0])
            flat = lambda x: x[:, :, :].rearrange("p i j -> p (i j)")
            did(nc.vector.tensor_tensor_scan(flat(exits), flat(left), flat(t1), 0.0, ALU.mult, ALU.add))

            for i in range(BR):
                old, new = maps[(i + 1) % 2], maps[i % 2]
                did(nc.vector.tensor_tensor(cand[0][:, :], up[:, i, :], old[:, 2:2 + L], ALU.mult))
                did(nc.vector.tensor_tensor(cand[1][:, :], dg[:, i, :], old[:, 1:1 + L], ALU.mult))
                dve.wait_ge(st, n[0])
                did(nc.vector.tensor_tensor(cand[2][:, :], cand[0][:, :], cand[1][:, :], ALU.add))
                dve.wait_ge(st, n[0])
                did(nc.vector.tensor_tensor_scan(new[:, 2:2 + L], left[:, i, :], cand[2][:, :], 0.0, ALU.mult,
                                                 ALU.add))
                dve.wait_ge(st, n[0])
            last = maps[(BR - 1) % 2]

            did(nc.vector.tensor_copy(entry[:, :], entry0[:, :]))
            for k in range(BLK - 1):
                dve.wait_ge(st, n[0])
                nc.vector.scalar_tensor_tensor(out=junk[0][:, :], in0=col[:, :], scalar=entry[:, :],
                                               in1=last[:, 2:2 + L], op0=ALU.is_equal, op1=ALU.mult,
                                               accum_out=found[:, :]).then_inc(gathered, 1)
                dve.wait_ge(shifted, k + 1)
                did(nc.vector.tensor_tensor(entry[:, :], s_ps[:, 0:1], entry0[:, :], ALU.add))
            dve.wait_ge(st, n[0])
            did(nc.vector.tensor_copy(hi[:, BR:BR + 1], entry[:, :]))

            for i in reversed(range(BR)):
                dve.wait_ge(st, n[0])
                did(nc.vector.scalar_tensor_tensor(out=junk[i % 2][:, :], in0=col[:, :], scalar=hi[:, 1 + i:2 + i],
                                                   in1=exits[:, i, :], op0=ALU.is_equal, op1=ALU.mult,
                                                   accum_out=ex[:, i:i + 1]))
                dve.wait_ge(st, n[0])
                did(nc.vector.tensor_scalar(off[:, i:i + 1], ex[:, i:i + 1], MARK, -(MARK + 1), ALU.is_ge, ALU.mult))
                dve.wait_ge(st, n[0])
                did(nc.vector.tensor_tensor(hi[:, i:i + 1], ex[:, i:i + 1], off[:, i:i + 1], ALU.add))
            dve.wait_ge(st, n[0])
            nc.vector.scalar_tensor_tensor(out=lo[:, :], in0=ex[:, :], scalar=MARK, in1=hi[:, 0:BR], op0=ALU.is_ge,
                                           op1=ALU.add).then_inc(gathered, 1)

            dve.wait_ge(turned, 2)
            for k in range(BLK):
                q, h = k % (P // BR), k // (P // BR)
                m = nc.vector.tensor_copy(K.hi[q * BR:(q + 1) * BR, h, :], hi_ps[0:BR, k * B:(k + 1) * B])
                m = nc.vector.tensor_copy(K.lo[q * BR:(q + 1) * BR, h, :], lo_ps[0:BR, k * B:(k + 1) * B])
            m.then_inc(spread, 1)

        @block.tensor
        def _(pe):
            pe.wait_ge(set_up, 1)
            for k in range(BLK - 1):
                pe.wait_ge(gathered, k + 1)
                nc.tensor.matmul(s_ps[:, 0:1], shift[:, :], found[:, :], start=True, stop=True).then_inc(shifted, 1)
            pe.wait_ge(gathered, BLK)
            nc.tensor.transpose(hi_ps[0:BR, 0:P], hi[:, 1:1 + BR], K.ident[:, :]).then_inc(turned, 1)
            nc.tensor.transpose(lo_ps[0:BR, 0:P], lo[:, :], K.ident[:, :]).then_inc(turned, 1)


def expand(K):
    nc, sem = K.nc, K.sem
    with ExitStack() as c:
        sb = lambda name, shape, dt=F32: c.enter_context(nc.sbuf_tensor(name, shape, dt))
        ps = lambda name, shape: c.enter_context(nc.psum_tensor(name, shape, F32))
        col = sb("ex_col", [P, L])
        upto = [sb(f"ex_upto{u}", [P, 2, L]) for u in range(2)]
        on = [sb(f"ex_on{u}", [P, 2, L]) for u in range(2)]
        stats = sb("ex_stats", [P, TT, 6])
        mv = sb("ex_mv", [P, TT, 2])
        var = sb("ex_var", [P, TT])
        rstd = sb("ex_rstd", [P, TT])
        nmr = sb("ex_nmr", [P, TT])
        xn = [sb(f"ex_xn{u}", [P, 2, D]) for u in range(2)]
        xt = [sb(f"ex_xt{u}", [P, DC, L]) for u in range(2)]
        logits = [sb(f"ex_logits{u}", [P, 2, E]) for u in range(2)]
        most = [sb(f"ex_most{u}", [P, 2, 8]) for u in range(2)]
        most_at = [sb(f"ex_most_at{u}", [P, 2, 8], U32) for u in range(2)]
        e_ps = [ps(f"ex_e{u}", [P, 2, D]) for u in range(2)]
        xt_ps = [ps(f"ex_xt_ps{u}", [P, DC, L]) for u in range(2)]
        l_ps = [ps(f"ex_l{u}", [P, 4, P]) for u in range(2)]

        col_ok = sem("ex_col_ok")
        half = sem("ex_half")
        mask = sem("ex_mask")
        e_mm, x_ok = sem("ex_e_mm"), sem("ex_x_ok")
        part = sem("ex_part")
        stt = sem("ex_stats_ok")
        root = sem("ex_root")
        xn_ok, t_ok, xt_ok, l_mm, l_ok = (sem("ex_" + x) for x in ("xn_ok", "t_ok", "xt_ok", "l_mm", "l_ok"))
        top = sem("ex_top")
        kept = sem("ex_kept")
        xn_out = [sem(f"ex_xn_out{u}") for u in range(2)]
        block = c.enter_context(nc.Block())
        tile = lambda buf, t: buf[:, bass.ds(t, 1), :].rearrange("p a d -> p (a d)")

        @block.sync
        def _(sp):
            for r in range(WRING):
                load_weights(K, sp, r, r)
            with sp.Fori(0, B // 2) as q:
                for u in range(2):
                    b = q * 2 + u
                    sp.wait_ge(xn_ok, b + 1)
                    sp.dma_start(K.xn_dram[bass.ds(b * L, L), :].rearrange("(t p) d -> p t d", p=P),
                                 xn[u][:, :, :]).then_inc(xn_out[u], 16)
            for u in range(2):
                sp.wait_ge(xn_out[u], 16 * (B // 2))

        @block.gpsimd
        def _(pool):
            nc.gpsimd.iota(col[:, :], [[1, L]], base=0, channel_multiplier=0,
                           allow_small_or_imprecise_dtypes=True).then_inc(col_ok, 1)

        @block.vector
        def _(dve):
            dve.wait_ge(col_ok, 1)

            def masks(b, u):
                dve.wait_ge(e_mm, b if u == 0 else b - 1)
                settle(dve)
                for h in range(2):
                    nc.vector.tensor_scalar(upto[u][:, h, :], col[:, :], K.hi[:, h, bass.ds(b, 1)], None,
                                            ALU.is_le).then_inc(half, 1)
                dve.wait_ge(half, b * 2 + 2)
                settle(dve)
                for h in range(2):
                    m = nc.vector.scalar_tensor_tensor(out=on[u][:, h, :], in0=col[:, :],
                                                       scalar=K.lo[:, h, bass.ds(b, 1)], in1=upto[u][:, h, :],
                                                       op0=ALU.is_ge, op1=ALU.mult)
                m.then_inc(mask, 1)

            def add(b, u):
                rows = K.x[:, bass.ds(b * 2, 2), :]
                dve.wait_ge(e_mm, b + 1)
                nc.vector.tensor_tensor(rows, rows, e_ps[u][:, :, :], ALU.add).then_inc(x_ok, 1)
                dve.wait_ge(x_ok, b + 1)
                settle(dve)
                for t in range(2):
                    m = nc.vector.bn_stats(tile(stats, b * 2 + t), tile(K.x, b * 2 + t))
                m.then_inc(part, 1)

            masks(0, 0)
            with dve.Fori(0, B // 2 - 1) as q:
                for u in range(2):
                    masks(q * 2 + u + 1, (u + 1) % 2)
                    add(q * 2 + u, u)
            masks(B - 1, 1)
            add(B - 2, 0)
            add(B - 1, 1)
            dve.wait_ge(part, B)
            for t in range(TT):
                m = nc.vector.bn_aggr(mv[:, t, :], stats[:, t, :])
            m.then_inc(stt, 1)
            dve.wait_ge(stt, 1)
            nc.vector.tensor_scalar(var[:, :], mv[:, :, 1], EPS, None, ALU.add).then_inc(stt, 1)
            dve.wait_ge(root, 1)
            refined_scales(dve, nc, stt, 2, mv, var, rstd, nmr)

            with dve.Fori(0, B // 2) as q:
                for u in range(2):
                    b = q * 2 + u
                    dve.wait_ge(t_ok, b + 1)
                    dve.wait_ge(l_mm, b if u == 0 else b - 1)
                    nc.vector.tensor_copy(xt[u][:, :, :], xt_ps[u][:, :, :]).then_inc(xt_ok, 1)
                    dve.wait_ge(l_ok, b + 1)
                    settle(dve)
                    for t in range(2):
                        m = nc.vector.max(most[u][:, t, :], logits[u][:, t, :])
                    m.then_inc(top, 1)
                    dve.wait_ge(top, b * 2 + 1)
                    settle(dve)
                    for t in range(2):
                        m = nc.vector.max_index(most_at[u][:, t, :], most[u][:, t, :], logits[u][:, t, :])
                    m.then_inc(top, 1)
                    dve.wait_ge(top, b * 2 + 2)
                    settle(dve)
                    nc.vector.tensor_copy(K.top[:, bass.ds(b * 2, 2), :], most[u][:, :, 0:2])
                    nc.vector.tensor_copy(K.top_at[:, bass.ds(b * 2, 2), :], most_at[u][:, :, 0:2]).then_inc(kept, 1)

        @block.scalar
        def _(act):
            act.wait_ge(stt, 2)
            nc.scalar.activation(mv[:, :, 1], var[:, :], ACT.Sqrt).then_inc(root, 1)
            act.wait_ge(stt, 8)

            with act.Fori(0, B // 2) as q:
                for u in range(2):
                    b = q * 2 + u
                    act.wait_ge(t_ok, b if u == 0 else b - 1)
                    act.wait_ge(xn_out[u], q * 16)
                    settle(act)
                    for t in range(2):
                        m = nc.scalar.activation(xn[u][:, t, :], tile(K.x, b * 2 + t), ACT.Identity,
                                                 bias=nmr[:, bass.ds(b * 2 + t, 1)],
                                                 scale=rstd[:, bass.ds(b * 2 + t, 1)])
                    m.then_inc(xn_ok, 1)
                    act.wait_ge(l_mm, b + 1)
                    act.wait_ge(kept, b if u == 0 else b - 1)
                    nc.scalar.activation(logits[u][:, :, :], l_ps[u][:, 0:2, 0:E],
                                         ACT.Copy).then_inc(l_ok, 1)

        @block.tensor
        def _(pe):
            with pe.Fori(0, B // 2) as q:
                for u in range(2):
                    b = q * 2 + u
                    pe.wait_ge(mask, b + 1)
                    pe.wait_ge(x_ok, b if u == 0 else b - 1)
                    for j in range(2):
                        for h in range(2):
                            m = nc.tensor.matmul(e_ps[u][:, j, :], on[u][:, h, j * P:(j + 1) * P],
                                                 tile(K.cx, b * 2 + h), start=(h == 0), stop=(h == 1))
                    m.then_inc(e_mm, 1)

            with pe.Fori(0, B // 2) as q:
                for u in range(2):
                    b = q * 2 + u
                    pe.wait_ge(xn_ok, b + 1)
                    pe.wait_ge(xt_ok, b if u == 0 else b - 1)
                    for t in range(2):
                        for c_ in range(DC):
                            m = nc.tensor.transpose(xt_ps[u][:, c_, t * P:(t + 1) * P],
                                                    xn[u][:, t, c_ * P:(c_ + 1) * P], K.ident[:, :])
                    m.then_inc(t_ok, 1)
                    pe.wait_ge(xt_ok, b + 1)
                    pe.wait_ge(l_ok, b if u == 0 else b - 1)
                    for t in range(2):
                        for c_ in range(DC):
                            m = nc.tensor.matmul(l_ps[u][:, t, 0:E], xt[u][:, c_, t * P:(t + 1) * P],
                                                 K.gate[:, c_, :], start=(c_ == 0), stop=(c_ == DC - 1))
                    m.then_inc(l_mm, 1)


def route(K):
    nc, sem = K.nc, K.sem
    with ExitStack() as c:
        sb = lambda name, shape, dt=F32: c.enter_context(nc.sbuf_tensor(name, shape, dt))
        ps = lambda name, shape: c.enter_context(nc.psum_tensor(name, shape, F32))
        expert = sb("ro_expert", [P, E])
        place = sb("ro_place", [P, MT + 1])
        token = sb("ro_token", [P, 2, TT])
        ones = sb("ro_ones", [P, P], BF16)
        after = sb("ro_after", [P, P], BF16)
        hot = [sb(f"ro_hot{i}", [P, TT, E]) for i in range(2)]
        chosen = sb("ro_chosen", [P, TT, E], BF16)
        upto = [sb(f"ro_upto{i}", [P, TT, E], BF16) for i in range(2)]
        picked = [sb(f"ro_picked{i}", [P, TT, E]) for i in range(2)]
        first = sb("ro_first", [P, TT, E])
        count = sb("ro_count", [P, E], I32)
        up = sb("ro_up", [P, E], I32)
        tiles = sb("ro_tiles", [P, E])
        one = sb("ro_one", [P, E])
        ends = sb("ro_ends", [P, E])
        start = sb("ro_start", [P, E])
        hi_i = sb("ro_hi_i", [P, 2, TT], I32)
        lo_i = sb("ro_lo_i", [P, 2, TT], I32)
        pos = sb("ro_pos", [P, 2, TT])
        hi = sb("ro_hi", [P, 2 * TT])
        lo = sb("ro_lo", [P, 2 * TT])
        gap = sb("ro_gap", [P, TT])
        ex = sb("ro_exp", [P, TT])
        ex1 = sb("ro_exp1", [P, TT])
        at_lo = [sb(f"ro_at_lo{i}", [P, P]) for i in range(4)]
        at_hi = [sb(f"ro_at_hi{i}", [P, MT + 1]) for i in range(4)]
        GT = TT // 4
        rank_ps = [ps(f"ro_rank{g}", [P, GT, E]) for g in range(4)]
        count_ps = ps("ro_count_ps", [P, 512])
        table_ps = ps("ro_table", [P, 512])
        set_up, raw = sem("ro_set_up"), sem("ro_raw")
        st = sem("ro_steps")
        sums = sem("ro_sums")
        exp_ok = sem("ro_exp_ok")
        gap_ok = sem("ro_gap_ok")
        ranks = sem("ro_ranks")
        marks = sem("ro_marks")
        used = sem("ro_used")
        tabled = sem("ro_tabled")
        block = c.enter_context(nc.Block())

        @block.gpsimd
        def _(pool):
            nc.gpsimd.memset(after[:, :], 0.0).then_inc(raw, 1)
            nc.gpsimd.memset(ones[:, :], 1.0).then_inc(set_up, 1)
            nc.gpsimd.memset(one[:, :], 1.0).then_inc(set_up, 1)
            nc.gpsimd.iota(expert[:, :], [[1, E]], base=0, channel_multiplier=0,
                           allow_small_or_imprecise_dtypes=True).then_inc(set_up, 1)
            nc.gpsimd.iota(place[:, :], [[1, MT + 1]], base=0, channel_multiplier=0,
                           allow_small_or_imprecise_dtypes=True).then_inc(set_up, 1)
            nc.gpsimd.iota(token[:, :, :], [[0, 2], [P, TT]], base=0, channel_multiplier=1,
                           allow_small_or_imprecise_dtypes=True).then_inc(set_up, 1)
            pool.wait_ge(raw, 1)
            nc.gpsimd.affine_select(out=after[:, :], in_=after[:, :], compare_op=ALU.is_gt, fill=-1.0, base=0,
                                    pattern=[[1, P]], channel_multiplier=-1).then_inc(set_up, 1)

        @block.scalar
        def _(act):
            act.wait_ge(gap_ok, 1)
            nc.scalar.activation(ex[:, :], gap[:, :], ACT.Exp).then_inc(exp_ok, 1)

        @block.vector
        def _(dve):
            n = [0]

            def did(ins):
                n[0] += 1
                ins.then_inc(st, 1)
                return ins

            dve.wait_ge(set_up, 6)
            nc.vector.tensor_tensor(gap[:, :], K.top[:, :, 1], K.top[:, :, 0], ALU.subtract).then_inc(gap_ok, 1)
            for i in range(2):
                did(nc.vector.tensor_tensor(hot[i][:, :, :],
                                            expert[:, :].rearrange("p (a e) -> p a e", a=1).broadcast_to([P, TT, E]),
                                            K.top_at[:, :, i:i + 1].broadcast_to([P, TT, E]), ALU.is_equal))
            dve.wait_ge(st, n[0])
            did(nc.vector.tensor_tensor(chosen[:, :, :], hot[0][:, :, :], hot[1][:, :, :], ALU.add))
            old, k, i = chosen, 1, 0
            while k < TT:
                dve.wait_ge(st, n[0])
                new = upto[i]
                did(nc.vector.tensor_tensor(new[:, k:, :], old[:, k:, :], old[:, :TT - k, :], ALU.add))
                did(nc.vector.tensor_copy(new[:, :k, :], old[:, :k, :]))
                old, k, i = new, 2 * k, 1 - i
            dve.wait_ge(st, n[0])
            K.sums_buf = old
            dve.sem_inc(sums, 1)
            dve.wait_ge(exp_ok, 1)
            did(nc.vector.tensor_scalar(ex1[:, :], ex[:, :], 1.0, None, ALU.add))
            dve.wait_ge(st, n[0])
            did(nc.vector.reciprocal(K.weight[:, 0, :], ex1[:, :]))
            dve.wait_ge(st, n[0])
            did(nc.vector.tensor_tensor(K.weight[:, 1, :], ex[:, :], K.weight[:, 0, :], ALU.mult))

            dve.wait_ge(ranks, 1)
            did(nc.vector.tensor_scalar(count[:, :], count_ps[:, 0:E], float(P - 1), None, ALU.add))
            dve.wait_ge(st, n[0])
            did(nc.vector.tensor_scalar(up[:, :], count[:, :], P.bit_length() - 1, None, ALU.arith_shift_right))
            dve.wait_ge(st, n[0])
            did(nc.vector.tensor_scalar(tiles[:, :], up[:, :], 1.0, None, ALU.max))
            dve.wait_ge(st, n[0])
            did(nc.vector.tensor_tensor_scan(ends[:, :], one[:, :], tiles[:, :], 0.0, ALU.mult, ALU.add))
            dve.wait_ge(st, n[0])
            did(nc.vector.tensor_tensor(start[:, :], ends[:, :], tiles[:, :], ALU.subtract))
            did(nc.vector.tensor_copy(K.tile_of[:, 1:E + 1], ends[:, :]))
            did(nc.vector.memset(K.tile_of[:, 0:1], 0))
            dve.wait_ge(st, n[0])
            did(nc.vector.tensor_scalar(start[:, :], start[:, :], float(P), None, ALU.mult))
            dve.wait_ge(st, n[0])
            for g in range(4):
                did(nc.vector.tensor_tensor(first[:, g * GT:(g + 1) * GT, :], rank_ps[g][:, :, :],
                                            start[:, :].rearrange("p (a e) -> p a e", a=1).broadcast_to([P, GT, E]),
                                            ALU.add))
            dve.wait_ge(st, n[0])
            for i in range(2):
                did(nc.vector.tensor_tensor(picked[i][:, :, :], hot[i][:, :, :], first[:, :, :], ALU.mult))
            dve.wait_ge(st, n[0])
            for i in range(2):
                did(nc.vector.tensor_reduce(pos[:, i, :], picked[i][:, :, :], AX_X, ALU.add))
            dve.wait_ge(st, n[0])
            did(nc.vector.tensor_copy(K.pos[:, :, :], pos[:, :, :]))
            dve.wait_ge(st, n[0])
            did(nc.vector.tensor_scalar(hi_i[:, :, :], K.pos[:, :, :], P.bit_length() - 1, None,
                                        ALU.arith_shift_right))
            did(nc.vector.tensor_scalar(lo_i[:, :, :], K.pos[:, :, :], P - 1, None, ALU.bitwise_and))
            dve.wait_ge(st, n[0])
            did(nc.vector.tensor_copy(hi[:, :], hi_i[:, :, :].rearrange("p s t -> p (s t)")))
            did(nc.vector.tensor_copy(lo[:, :], lo_i[:, :, :].rearrange("p s t -> p (s t)")))
            dve.wait_ge(st, n[0])
            tok = token[:, :, :].rearrange("p s t -> p (s t)")
            with dve.Fori(0, 2 * TT // 4) as q:
                for u in range(4):
                    k = q * 4 + u
                    dve.wait_ge(used, k + 1)
                    settle(dve)
                    nc.vector.tensor_scalar(at_lo[u][:, :], place[:, 0:P], lo[:, bass.ds(k, 1)], None,
                                            ALU.is_equal).then_inc(marks, 1)
                    nc.vector.tensor_scalar(at_hi[u][:, :], place[:, :], hi[:, bass.ds(k, 1)], tok[:, bass.ds(k, 1)],
                                            ALU.is_equal, ALU.mult).then_inc(marks, 1)
            dve.wait_ge(tabled, 1)
            nc.vector.tensor_copy(K.table[:, :], table_ps[:, 0:MT + 1]).then_inc(st, 1)

        @block.tensor
        def _(pe):
            pe.sem_inc(used, 4)
            pe.wait_ge(set_up, 6)
            pe.wait_ge(sums, 1)
            upto_last = K.sums_buf
            nc.tensor.matmul(count_ps[:, 0:E], ones[:, :], upto_last[:, TT - 1, :], start=True, stop=True)
            for g in range(4):
                rows = slice(g * GT, (g + 1) * GT)
                nc.tensor.matmul(rank_ps[g][:, :, :], ones[:, :], upto_last[:, rows, :], start=True, stop=False)
                m = nc.tensor.matmul(rank_ps[g][:, :, :], after[:, :], chosen[:, rows, :], start=False, stop=True)
            m.then_inc(ranks, 1)

            def enter(k, u, start=False, stop=False):
                pe.wait_ge(marks, 2 * k + 2)
                m = nc.tensor.matmul(table_ps[:, 0:MT + 1], at_lo[u][:, :], at_hi[u][:, :], start=start, stop=stop)
                m.then_inc(used, 1)
                return m

            for u in range(4):
                enter(u, u, start=(u == 0))
            with pe.Fori(1, 2 * TT // 4 - 1) as q:
                for u in range(4):
                    enter(q * 4 + u, u)
            for u in range(4):
                m = enter(2 * TT - 4 + u, u, stop=(u == 3))
            pe.wait_ge(used, 4 + 2 * TT)
            pe.sem_inc(tabled, 1)


def load_weights(K, sp, e, r):
    one = lambda w: w[bass.ds(e, 1), :, :].rearrange("a (c p) f -> p (a c) f", p=P)
    for w, dram in zip(K.w[r], (K.w0_dram, K.w1_dram, K.wo_dram)):
        sp.dma_start(w[:, :, :], one(dram)).then_inc(K.w_in[r], 16)


def experts(K):
    nc, sem = K.nc, K.sem
    with ExitStack() as c:
        sb = lambda name, shape, dt=F32: c.enter_context(nc.sbuf_tensor(name, shape, dt))
        ps = lambda name, shape: c.enter_context(nc.psum_tensor(name, shape, F32))
        index = sb("mo_index", [P, 1], I32)
        index_ok = sem("mo_index_ok")
        xg = sb("mo_xg", [P, D])
        xt = sb("mo_xt", [P, DC, P])
        silu = [sb(f"mo_silu{m}", [P, P]) for m in range(FC)]
        inter = [sb(f"mo_inter{m}", [P, P]) for m in range(FC)]
        o_sb = sb("mo_o", [P, D])
        h_ps = [ps(f"mo_h{m}", [P, 512]) for m in range(FC)]
        xt_ps = ps("mo_xt_ps", [P, 512])
        o_ps = ps("mo_o_ps", [P, 512])
        x_in = sem("mo_x_in")
        turned = sem("mo_turned")
        xt_ok = sem("mo_xt_ok")
        up_mm = sem("mo_up")
        silu_ok = sem("mo_silu_ok")
        inter_ok = sem("mo_inter_ok")
        down_mm = sem("mo_down")
        o_ok = sem("mo_o_ok")
        o_out = sem("mo_o_out")
        w_used = sem("mo_w_used")
        block = c.enter_context(nc.Block())

        def tile_no(eng, e):
            return eng.value_load(K.tile_of[0:1, bass.ds(e, 1)], min_val=0, max_val=MT)

        @block.sync
        def _(sp):
            with sp.Fori(1, E // WRING) as q:
                for r in range(WRING):
                    sp.wait_ge(w_used, (q - 1) * WRING + r + 1)
                    load_weights(K, sp, q * WRING + r, r)

        @block.gpsimd
        def _(pool):
            end = tile_no(pool, E)
            with pool.Fori(0, end + 1) as g:
                pool.wait_ge(x_in, g * 16)
                settle(pool)
                nc.gpsimd.tensor_copy(index[:, :], K.table[:, bass.ds(g, 1)]).then_inc(index_ok, 1)
                pool.wait_ge(index_ok, g + 1)
                pool.wait_ge(turned, g)
                settle(pool)
                nc.gpsimd.indirect_dma_start(xg[:, :], None, K.xn_dram[:, :],
                                             bass.IndirectOffsetOnAxis(ap=index[:, :], axis=0)
                                             ).then_inc(x_in, 16)

        @block.tensor
        def _(pe):
            pe.sem_inc(down_mm, FC)

            def turn(g):
                pe.wait_ge(x_in, (g + 1) * 16)
                for c_ in range(DC):
                    m = nc.tensor.transpose(xt_ps[:, c_ * P:(c_ + 1) * P], xg[:, c_ * P:(c_ + 1) * P], K.ident[:, :])
                m.then_inc(turned, 1)

            def up(g, r, m):
                pe.wait_ge(inter_ok, g * FC + (m + 1))
                for i in range(2):
                    for c_ in range(DC):
                        ins = nc.tensor.matmul(h_ps[m][:, i * P:(i + 1) * P], K.w[r][i][:, c_, m * P:(m + 1) * P],
                                               xt[:, c_, :], start=(c_ == 0), stop=(c_ == DC - 1))
                ins.then_inc(up_mm, 1)

            def down(g, r, m):
                pe.wait_ge(inter_ok, g * FC + (FC + m + 1))
                if m == 0:
                    pe.wait_ge(o_ok, g)
                nc.tensor.matmul(o_ps[:, 0:D], inter[m][:, :], K.w[r][2][:, m, :], start=(m == 0),
                                 stop=(m == FC - 1)).then_inc(down_mm, 1)

            turn(0)
            with pe.Fori(0, E // WRING) as q:
                for r in range(WRING):
                    e = q * WRING + r
                    first, end = tile_no(pe, e), tile_no(pe, e + 1)
                    pe.wait_ge(K.w_in[r], q * 48 + 48)
                    settle(pe)
                    with pe.Fori(first, end) as g:
                        pe.wait_ge(xt_ok, g + 1)
                        up(g, r, 0)
                        up(g, r, 1)
                        down(g, r, 0)
                        up(g, r, 2)
                        down(g, r, 1)
                        up(g, r, 3)
                        turn(g + 1)
                        down(g, r, 2)
                        down(g, r, 3)
                    pe.wait_ge(down_mm, end * FC + FC)
                    pe.sem_inc(w_used, 1)

        @block.scalar
        def _(act):
            end = tile_no(act, E)
            with act.Fori(0, end) as g:
                for m in range(FC):
                    act.wait_ge(up_mm, g * FC + (m + 1))
                    act.wait_ge(inter_ok, g * FC + (m + 1))
                    nc.scalar.activation(silu[m][:, :], h_ps[m][:, 0:P], ACT.Silu).then_inc(silu_ok, 1)
                act.wait_ge(o_ok, g + 1)
                act.dma_start(K.outs_dram[bass.ds(g * P, P), :], o_sb[:, :]).then_inc(o_out, 16)
            act.wait_ge(o_out, end * 16)
            settle(act)

        @block.vector
        def _(dve):
            dve.sem_inc(inter_ok, FC)

            def take_turned(g):
                dve.wait_ge(turned, g + 1)
                nc.vector.tensor_copy(xt[:, :, :], xt_ps[:, 0:D].rearrange("p (c t) -> p c t", c=DC)
                                      ).then_inc(xt_ok, 1)

            take_turned(0)
            end = tile_no(dve, E)
            with dve.Fori(0, end) as g:
                for m in range(FC):
                    dve.wait_ge(silu_ok, g * FC + (m + 1))
                    dve.wait_ge(down_mm, g * FC + (m + 1))
                    nc.vector.tensor_tensor(inter[m][:, :], silu[m][:, :], h_ps[m][:, P:2 * P],
                                            ALU.mult).then_inc(inter_ok, 1)
                take_turned(g + 1)
                dve.wait_ge(down_mm, g * FC + 2 * FC)
                dve.wait_ge(o_out, g * 16)
                nc.vector.tensor_copy(o_sb[:, :], o_ps[:, 0:D]).then_inc(o_ok, 1)


def combine(K):
    nc, sem = K.nc, K.sem
    RING = 4
    with ExitStack() as c:
        got = [[c.enter_context(nc.sbuf_tensor(f"co_got{u}_{i}", [P, D], F32)) for i in range(2)] for u in range(RING)]
        index = [c.enter_context(nc.sbuf_tensor(f"co_index{u}", [P, 2], I32)) for u in range(RING)]
        index_ok = sem("co_index_ok")
        got_in = [sem(f"co_got_in{u}") for u in range(RING)]
        added = sem("co_added")
        out = sem("co_out")
        block = c.enter_context(nc.Block())
        tile = lambda t: K.x[:, bass.ds(t, 1), :].rearrange("p a d -> p (a d)")

        @block.gpsimd
        def _(pool):
            with pool.Fori(0, TT // RING) as q:
                for u in range(RING):
                    t = q * RING + u
                    pool.wait_ge(added, t * 2 + 2)
                    settle(pool)
                    nc.gpsimd.tensor_copy(index[u][:, :], K.pos[:, :, bass.ds(t, 1)].rearrange("p i a -> p (i a)")
                                          ).then_inc(index_ok, 1)
                    pool.wait_ge(index_ok, t + 1)
                    settle(pool)
                    for i in range(2):
                        nc.gpsimd.indirect_dma_start(got[u][i][:, :], None, K.outs_dram[:, :],
                                                     bass.IndirectOffsetOnAxis(ap=index[u][:, i:i + 1], axis=0)
                                                     ).then_inc(got_in[u], 16)

        @block.vector
        def _(dve):
            dve.sem_inc(added, 2 * RING)
            with dve.Fori(0, TT // RING) as q:
                for u in range(RING):
                    t = q * RING + u
                    dve.wait_ge(got_in[u], q * 32 + 32)
                    for i in range(2):
                        if i:
                            dve.wait_ge(added, t * 2 + (2 * RING + 1))
                        settle(dve)
                        nc.vector.scalar_tensor_tensor(out=tile(t), in0=got[u][i][:, :],
                                                       scalar=K.weight[:, i, bass.ds(t, 1)], in1=tile(t),
                                                       op0=ALU.mult, op1=ALU.add).then_inc(added, 1)

        @block.sync
        def _(sp):
            with sp.Fori(0, TT // RING) as q:
                sp.wait_ge(added, q * 2 * RING + 4 * RING)
                sp.dma_start(K.out_dram[bass.ds(q * RING * P, RING * P), :].rearrange("(t p) d -> p t d", p=P),
                             K.x[:, bass.ds(q * RING, RING), :]).then_inc(out, 16)
            sp.wait_ge(out, TT // RING * 16)


def build(nc, x, ctx_in, a_log, w_delta, w_dt, b_dt, w_b, w_c, d_skip, gate, w0, w1, wo, out):
    K = Chip()
    K.nc = nc
    with ExitStack() as ctx:
        K.ctx = ctx
        sb = lambda name, shape, dt=F32: ctx.enter_context(nc.sbuf_tensor(name, shape, dt))
        K.sem = lambda name: ctx.enter_context(nc.semaphore(name))
        K.dist_dram = nc.dram_tensor("dist", (B, L, L), F32, kind="Internal").ap()
        K.xn_dram = nc.dram_tensor("xn", (TOK, D), F32, kind="Internal").ap()
        K.outs_dram = nc.dram_tensor("outs", (MT * P, D), F32, kind="Internal").ap()
        K.x_dram = x.rearrange("b l d -> (b l) d")
        K.ctx_dram = ctx_in
        K.a_log_dram, K.w_delta_dram, K.w_dt_dram, K.b_dt_dram = a_log, w_delta, w_dt, b_dt
        K.w_b_dram, K.w_c_dram, K.d_skip_dram, K.gate_dram = w_b, w_c, d_skip, gate
        K.w0_dram, K.w1_dram, K.wo_dram = w0, w1, wo
        K.out_dram = out.rearrange("b l d -> (b l) d")

        K.x = sb("x", [P, TT, D])
        K.ident = sb("ident", [P, P])
        K.gate = sb("gate", [P, DC, E])
        K.hi = sb("hi", [P, 2, B])
        K.lo = sb("lo", [P, 2, B])

        K.codes = sb("codes", [P, SEG, BR, 2, SW], F16)
        K.cx = K.codes[:, :, :, :, :].rearrange("p s i a j -> p (s i a j)").bitcast(F32).rearrange(
            "p (t d) -> p t d", d=D)
        with ExitStack() as c_wave:
            K.wave = c_wave.enter_context(nc.sbuf_tensor("wave", [P, STEPS * SW], F32))
            with ExitStack() as ssm:
                sb2 = lambda name, shape, dt=F32: ssm.enter_context(nc.sbuf_tensor(name, shape, dt))
                K.rstd = sb2("rstd", [P, TT])
                K.nmr = sb2("nmr", [P, TT])
                K.a_neg = sb2("a_neg", [P, DC, N])
                K.w_delta = sb2("w_delta", [P, DC, R])
                K.w_dt = sb2("w_dt", [R, D])
                K.b_dt = sb2("b_dt", [P, DC])
                K.d_skip = sb2("d_skip", [P, DC])
                K.w_bc = sb2("w_bc", [P, DC, 2 * N])
                K.xt = sb2("xt", [P, DC, TOK])
                K.delta = sb2("delta", [P, DC, TOK])
                K.dx = K.wave[:, 0:DC * TOK].rearrange("p (c t) -> p c t", c=DC)
                spare = K.codes[:, :, :, :, :].rearrange("p s i a j -> p (s i a j)").bitcast(BF16)
                K.bc3 = spare[0:6 * N, 0:TOK]
                K.bc_sel = spare[0:6 * N, TOK:TOK + 2 * N * P].rearrange("p (m q) -> p m q", q=P)
                run(K, load_and_constants, prepare, scan_states, distances)
            run(K, wave)
        run(K, trace_back)
        sb3 = lambda name, shape, dt=F32: ctx.enter_context(nc.sbuf_tensor(name, shape, dt))
        K.w = [[sb3(f"w0_{r}", [P, DC, F]), sb3(f"w1_{r}", [P, DC, F]), sb3(f"wo_{r}", [P, FC, D])]
               for r in range(WRING)]
        K.w_in = [K.sem(f"w_in{r}") for r in range(WRING)]
        K.top = sb3("top", [P, TT, 2])
        K.top_at = sb3("top_at", [P, TT, 2])
        K.weight = sb3("weight", [P, 2, TT])
        K.pos = sb3("pos", [P, 2, TT], I32)
        K.tile_of = sb3("tile_of", [P, E + 1], I32)
        K.table = sb3("table", [P, MT + 1], I32)
        run(K, expand)
        run(K, route, experts, combine)


_INS = ['x', 'ctx_1024', 'L0_attn_A_log', 'L0_attn_W_delta', 'L0_attn_W_dt', 'L0_attn_b_dt', 'L0_attn_W_B',
        'L0_attn_W_C', 'L0_attn_D', 'L0_ffn_gate_kernel', 'L0_ffn_w0', 'L0_ffn_w1', 'L0_ffn_wo']
_OUTS = [((B, L, D), 'float32')]


def kernel(**inputs):
    import numpy as _np
    import concourse.bacc as _bacc
    from concourse import mybir as _mybir
    from concourse.bass_utils import run_bass_kernel_spmd as _run

    nc = _bacc.Bacc("TRN2", target_bir_lowering=False, num_devices=1)
    arrays, args = {}, []
    for name in _INS:
        a = _np.ascontiguousarray(inputs[name])
        arrays[f"in_{name}_dram"] = a
        args.append(nc.dram_tensor(f"in_{name}_dram", a.shape, _mybir.dt.from_np(a.dtype), kind="ExternalInput").ap())
    for i, (shape, dtype) in enumerate(_OUTS):
        dt = _mybir.dt.from_np(_np.dtype(dtype))
        args.append(nc.dram_tensor(f"out_{i}_dram", shape, dt, kind="ExternalOutput").ap())
    build(nc, *args)
    r = _run(nc, [arrays], core_ids=[0])
    got = tuple(r.results[0][f"out_{i}_dram"] for i in range(len(_OUTS)))
    return got[0]
```

```python
from contextlib import ExitStack

import concourse.bass as bass
from concourse import mybir

ALU = mybir.AluOpType
ACT = mybir.ActivationFunctionType
AX_X = mybir.AxisListType.X
F32 = mybir.dt.float32
F16 = mybir.dt.float16
BF16 = mybir.dt.bfloat16
I32 = mybir.dt.int32
U32 = mybir.dt.uint32

P = 128
B, L, D = 16, 256, 256
N = 16
R = 64
E, F = 64, 512
DC = D // P
FC = F // P
TOK = B * L
TT = TOK // P
NP = B // 2
PT = 2 * L
PTT = PT // P
EPS = 1e-5
BIG = 1e30
SEG = 8
SW = L // SEG
LAG = 4
STEPS = L + LAG * (SEG - 1)
BLK = 8
BR = L // BLK
assert SEG * B == P and BLK * B == P
WRING = 4
MT = E + 2 * TOK // P
SPAN = 2 * MT
assert SPAN & (SPAN - 1) == 0


class Chip:
    pass


def run(K, *stages):
    for stage in stages:
        with ExitStack() as K.ctx:
            stage(K)


def settle(eng):
    eng.nop(nofuse=True)


START = 2


def start(eng, *sems):
    for s in sems:
        eng.sem_inc(s, START)


def after(i):
    return i + (1 + START)


def pair_exists(p):
    return not isinstance(p, int) or p < NP


def over_pairs(eng, body):
    with eng.Fori(0, NP // 2 - 1) as q:
        for u in range(2):
            body(q, u)
    for u in range(2):
        body(NP // 2 - 1, u)


def batch_exists(b):
    return not isinstance(b, int) or b < B


def over_batches(eng, body):
    with eng.Fori(0, B // 4 - 1) as q:
        for u in range(4):
            body(q, u)
    for u in range(4):
        body(B // 4 - 1, u)


def tile_stats(dve, nc, sem, count, tiles, stats, mv):
    settle(dve)
    for t, tile in enumerate(tiles):
        m = nc.vector.bn_stats(stats[:, t, :], tile)
    m.then_inc(sem, 1)
    dve.wait_ge(sem, count + 1)
    settle(dve)
    for t in range(len(tiles)):
        m = nc.vector.bn_aggr(mv[:, t, :], stats[:, t, :])
    m.then_inc(sem, 1)


def refined_scales(dve, nc, sem, count, mv, var, rstd, nmr):
    r, t = rstd[:, :], nmr[:, :]
    nc.vector.reciprocal(r, mv[:, :, 1]).then_inc(sem, 1)
    dve.wait_ge(sem, count + 1)
    nc.vector.tensor_tensor(t, r, r, ALU.mult).then_inc(sem, 1)
    dve.wait_ge(sem, count + 2)
    nc.vector.tensor_tensor(t, t, var[:, :], ALU.mult).then_inc(sem, 1)
    dve.wait_ge(sem, count + 3)
    nc.vector.tensor_scalar(t, t, -0.5, 1.5, ALU.mult, ALU.add).then_inc(sem, 1)
    dve.wait_ge(sem, count + 4)
    nc.vector.tensor_tensor(r, r, t, ALU.mult).then_inc(sem, 1)
    dve.wait_ge(sem, count + 5)
    nc.vector.scalar_tensor_tensor(out=t, in0=mv[:, :, 0], scalar=-1.0, in1=r, op0=ALU.mult,
                                   op1=ALU.mult).then_inc(sem, 1)


def load_and_constants(K):
    nc, sem = K.nc, K.sem
    w_in = sem("w_in")
    a_in = sem("a_in")
    a_exp = sem("a_exp")
    ident0 = sem("ident0")
    sel0 = sem("sel0")
    consts = sem("consts")
    x_in = [sem(f"x_in{g}") for g in range(NP)]
    st = sem("ln1_stats")
    root = sem("ln1_root")
    stats = K.ctx.enter_context(nc.sbuf_tensor("ln1_stats_sb", [P, TT, 6], F32))
    mv = K.ctx.enter_context(nc.sbuf_tensor("ln1_mv", [P, TT, 2], F32))
    var = K.ctx.enter_context(nc.sbuf_tensor("ln1_var", [P, TT], F32))

    block = K.ctx.enter_context(nc.Block())

    @block.sync
    def _(sp):
        for g in range(NP):
            sp.dma_start(K.x[:, g * PTT:(g + 1) * PTT, :],
                         K.x_dram[g * PT:(g + 1) * PT, :].rearrange("(t p) d -> p t d", p=P)).then_inc(x_in[g], 16)

    @block.scalar
    def _(act):
        act.dma_start(K.a_neg[:, :, :], K.a_log_dram.rearrange("(c p) n -> p c n", p=P)).then_inc(a_in, 16)
        act.dma_start(K.w_delta[:, :, :], K.w_delta_dram.rearrange("(c p) r -> p c r", p=P)).then_inc(w_in, 16)
        act.dma_start(K.w_dt[:, :], K.w_dt_dram).then_inc(w_in, 16)
        act.dma_start(K.b_dt[:, :], K.b_dt_dram.rearrange("(c p) -> p c", p=P),
                      allow_slow_non_contiguous=True).then_inc(w_in, 16)
        act.dma_start(K.d_skip[:, :], K.d_skip_dram.rearrange("(c p) -> p c", p=P),
                      allow_slow_non_contiguous=True).then_inc(w_in, 16)
        act.dma_start(K.w_bc[:, :, 0:N], K.w_b_dram.rearrange("(c p) n -> p c n", p=P)).then_inc(w_in, 16)
        act.dma_start(K.w_bc[:, :, N:2 * N], K.w_c_dram.rearrange("(c p) n -> p c n", p=P)).then_inc(w_in, 16)
        act.dma_start(K.gate[:, :, :], K.gate_dram.rearrange("(c p) e -> p c e", p=P)).then_inc(w_in, 16)
        act.wait_ge(a_in, 16)
        nc.scalar.activation(K.a_neg[:, :, :], K.a_neg[:, :, :], ACT.Exp).then_inc(a_exp, 1)
        act.wait_ge(w_in, 16 * 7)
        act.wait_ge(st, NP * 2 + 1)
        nc.scalar.activation(mv[:, :, 1], var[:, :], ACT.Sqrt).then_inc(root, 1)

    @block.vector
    def _(dve):
        for g in range(NP):
            dve.wait_ge(x_in[g], 16)
            tile_stats(dve, nc, st, g * 2, [K.x[:, g * PTT + t, :] for t in range(PTT)],
                       stats[:, g * PTT:(g + 1) * PTT, :], mv[:, g * PTT:(g + 1) * PTT, :])
        dve.wait_ge(st, NP * 2)
        nc.vector.tensor_scalar(var[:, :], mv[:, :, 1], EPS, None, ALU.add).then_inc(st, 1)
        dve.wait_ge(root, 1)
        refined_scales(dve, nc, st, NP * 2 + 1, mv, var, K.rstd, K.nmr)
        dve.wait_ge(a_exp, 1)
        nc.vector.tensor_scalar(K.a_neg[:, :, :], K.a_neg[:, :, :], -1.0, None, ALU.mult).then_inc(consts, 1)

    @block.gpsimd
    def _(pool):
        nc.gpsimd.memset(K.ident[:, :], 0.0).then_inc(ident0, 1)
        nc.gpsimd.memset(K.bc_sel[:, :, :], 0.0).then_inc(sel0, 1)
        pool.wait_ge(ident0, 1)
        nc.gpsimd.affine_select(out=K.ident[:, :], in_=K.ident[:, :], compare_op=ALU.not_equal, fill=1.0, base=0,
                                pattern=[[-1, P]], channel_multiplier=1).then_inc(consts, 1)
        for q in range(3):
            pool.wait_ge(sel0, q + 1)
            nc.gpsimd.affine_select(out=K.bc_sel[:, :, :], in_=K.bc_sel[:, :, :], compare_op=ALU.not_equal,
                                    fill=1.0, base=-2 * N * q, pattern=[[-1, 2 * N], [0, P]],
                                    channel_multiplier=1).then_inc(sel0, 1)


def prepare(K):
    nc, sem = K.nc, K.sem
    with ExitStack() as c:
        sb = lambda name, shape, dt=F32: c.enter_context(nc.sbuf_tensor(name, shape, dt))
        ps = lambda name, shape: c.enter_context(nc.psum_tensor(name, shape, F32))
        xn = [sb(f"pr_xn{u}", [P, PTT, D]) for u in range(2)]
        low = sb("pr_low", [R, PT])
        z_sb = sb("pr_z_sb", [P, DC, PT])
        az = sb("pr_az", [P, DC, PT])
        uz = az
        ez = sb("pr_ez", [P, DC, PT])
        lz = sb("pr_lz", [P, DC, PT])
        mz = sb("pr_mz", [P, DC, PT])
        cz = sb("pr_cz", [P, DC, PT])
        rest = sb("pr_rest", [2 * N, PT])
        mid = sb("pr_mid", [2 * N, PT], BF16)
        hi = sb("pr_hi", [2 * N, PT], BF16)
        xt_ps = [ps(f"pr_xt{u}", [P, DC, PT]) for u in range(2)]
        low_ps = ps("pr_low_ps", [P, PT])
        z_ps = ps("pr_z", [P, DC, PT])
        bc_ps = ps("pr_bc", [P, PT])

        norm = sem("pr_norm")
        turned = sem("pr_turned")
        xt_ok = sem("pr_xt_ok")
        low_mm, low_ok = sem("pr_low_mm"), sem("pr_low_ok")
        z_mm, z_ok = sem("pr_z_mm"), sem("pr_z_ok")
        bc_mm = sem("pr_bc_mm")
        d_max, d_abs, d_u, d_c = sem("pr_max"), sem("pr_abs"), sem("pr_u"), sem("pr_c")
        a_exp, a_ln = sem("pr_exp"), sem("pr_ln")
        p_s, p_delta, p_dx = sem("pr_s"), sem("pr_delta"), sem("pr_dx")
        s_hi, s_rest, s_mid, s_lo, s_midc, s_hic = (sem("pr_" + x) for x in ("hi", "rst", "mid", "lo", "midc", "hic"))
        block = c.enter_context(nc.Block())

        @block.vector
        def _(dve):
            start(dve, xt_ok, s_rest, s_lo, d_max, d_abs, d_u, d_c)

            def take_turned(p, u):
                dve.wait_ge(turned, after(p))
                settle(dve)
                nc.vector.tensor_copy(K.xt[:, :, bass.ds(p * PT, PT)], xt_ps[u][:, :, :]).then_inc(xt_ok, 1)

            def pair(q, u):
                p = q * 2 + u
                dve.wait_ge(bc_mm, after(p))
                dve.wait_ge(s_hi, after(p))
                dve.wait_ge(s_mid, after(p - 1))
                dve.wait_ge(s_lo, after(p - 1))
                nc.vector.tensor_tensor(rest[:, :], bc_ps[0:2 * N, :], hi[:, :], ALU.subtract).then_inc(s_rest, 1)
                if pair_exists(p + 1):
                    take_turned(p + 1, 1 - u)
                dve.wait_ge(s_mid, after(p))
                settle(dve)
                nc.vector.tensor_tensor(K.bc3[4 * N:6 * N, bass.ds(p * PT, PT)], rest[:, :], mid[:, :],
                                        ALU.subtract).then_inc(s_lo, 1)
                dve.wait_ge(z_ok, after(p))
                dve.wait_ge(d_c, after(p - 1))
                nc.vector.scalar_tensor_tensor(out=az[:, :, :], in0=z_sb[:, :, :], scalar=-1.0, in1=z_sb[:, :, :],
                                               op0=ALU.mult, op1=ALU.max).then_inc(d_abs, 1)
                dve.wait_ge(p_delta, after(p - 1))
                nc.vector.tensor_scalar(mz[:, :, :], z_sb[:, :, :], 0.0, None, ALU.max).then_inc(d_max, 1)
                dve.wait_ge(a_exp, after(p))
                nc.vector.tensor_scalar(uz[:, :, :], ez[:, :, :], 1.0, None, ALU.add).then_inc(d_u, 1)
                dve.wait_ge(d_u, after(p))
                dve.wait_ge(p_s, after(p - 1))
                nc.vector.scalar_tensor_tensor(out=cz[:, :, :], in0=uz[:, :, :], scalar=-1.0, in1=ez[:, :, :],
                                               op0=ALU.add, op1=ALU.subtract).then_inc(d_c, 1)

            take_turned(0, 0)
            over_pairs(dve, pair)

        @block.scalar
        def _(act):
            start(act, norm, low_ok, s_hi, s_hic, s_mid, s_midc, z_ok, a_exp, a_ln)
            nc.scalar.preload_act_table_set("natural_log_exp_and_others")

            def normalize(p, u):
                act.wait_ge(turned, after(p - 2))
                settle(act)
                for t in range(PTT):
                    m = nc.scalar.activation(xn[u][:, t, :],
                                             K.x[:, bass.ds(p * PTT + t, 1), :].rearrange("p a d -> p (a d)"),
                                             ACT.Identity, bias=K.nmr[:, bass.ds(p * PTT + t, 1)],
                                             scale=K.rstd[:, bass.ds(p * PTT + t, 1)])
                m.then_inc(norm, 1)

            def pair(q, u):
                p = q * 2 + u
                cols = bass.ds(p * PT, PT)
                act.wait_ge(low_mm, after(p))
                act.wait_ge(z_mm, after(p - 1))
                nc.scalar.activation(low[:, :], low_ps[0:R, :], ACT.Copy).then_inc(low_ok, 1)
                act.wait_ge(bc_mm, after(p))
                act.wait_ge(s_rest, after(p - 1))
                act.wait_ge(s_hic, after(p - 1))
                nc.scalar.activation(hi[:, :], bc_ps[0:2 * N, :], ACT.Copy).then_inc(s_hi, 1)
                if pair_exists(p + 2):
                    normalize(p + 2, u)
                act.wait_ge(s_hi, after(p))
                settle(act)
                nc.scalar.activation(K.bc3[0:2 * N, cols], hi[:, :], ACT.Copy).then_inc(s_hic, 1)
                act.wait_ge(s_rest, after(p))
                act.wait_ge(s_midc, after(p - 1))
                act.wait_ge(s_lo, after(p - 1))
                nc.scalar.activation(mid[:, :], rest[:, :], ACT.Copy).then_inc(s_mid, 1)
                act.wait_ge(z_mm, after(p))
                act.wait_ge(d_max, after(p - 1))
                act.wait_ge(d_abs, after(p - 1))
                for c_ in range(DC):
                    m = nc.scalar.activation(z_sb[:, c_, :], z_ps[:, c_, :], ACT.Identity, bias=K.b_dt[:, c_:c_ + 1])
                m.then_inc(z_ok, 1)
                act.wait_ge(s_mid, after(p))
                settle(act)
                nc.scalar.activation(K.bc3[2 * N:4 * N, cols], mid[:, :], ACT.Copy).then_inc(s_midc, 1)
                act.wait_ge(d_abs, after(p))
                act.wait_ge(d_c, after(p - 1))
                nc.scalar.activation(ez[:, :, :], az[:, :, :], ACT.Exp, scale=-1.0).then_inc(a_exp, 1)
                act.wait_ge(a_exp, after(p))
                act.wait_ge(p_s, after(p - 1))
                nc.scalar.activation(lz[:, :, :], ez[:, :, :], ACT.Ln, bias=1.0).then_inc(a_ln, 1)

            normalize(0, 0)
            normalize(1, 1)
            over_pairs(act, pair)

        @block.gpsimd
        def _(pool):
            start(pool, p_s, p_delta, p_dx)

            def pair(q, u):
                p = q * 2 + u
                cols = bass.ds(p * PT, PT)
                pool.wait_ge(a_ln, after(p))
                pool.wait_ge(d_c, after(p))
                settle(pool)
                nc.gpsimd.tensor_tensor(K.delta[:, :, cols], lz[:, :, :], cz[:, :, :], ALU.subtract).then_inc(p_s, 1)
                pool.wait_ge(p_s, after(p))
                pool.wait_ge(d_max, after(p))
                settle(pool)
                nc.gpsimd.tensor_tensor(K.delta[:, :, cols], K.delta[:, :, cols], mz[:, :, :],
                                        ALU.add).then_inc(p_delta, 1)
                pool.wait_ge(p_delta, after(p))
                pool.wait_ge(xt_ok, after(p))
                settle(pool)
                nc.gpsimd.tensor_tensor(K.dx[:, :, cols], K.delta[:, :, cols], K.xt[:, :, cols],
                                        ALU.mult).then_inc(p_dx, 1)

            over_pairs(pool, pair)

        @block.tensor
        def _(pe):
            start(pe, turned, low_mm, bc_mm, z_mm)

            def turn(p, u):
                pe.wait_ge(norm, after(p))
                pe.wait_ge(xt_ok, after(p - 2))
                for c_ in range(DC):
                    for t in range(PTT):
                        m = nc.tensor.transpose(xt_ps[u][:, c_, t * P:(t + 1) * P],
                                                xn[u][:, t, c_ * P:(c_ + 1) * P], K.ident[:, :])
                m.then_inc(turned, 1)

            def pair(q, u):
                p = q * 2 + u
                cols = bass.ds(p * PT, PT)
                pe.wait_ge(xt_ok, after(p))
                pe.wait_ge(low_ok, after(p - 1))
                for c_ in range(DC):
                    m = nc.tensor.matmul(low_ps[0:R, :], K.w_delta[:, c_, :], K.xt[:, c_, cols],
                                         start=(c_ == 0), stop=(c_ == DC - 1))
                m.then_inc(low_mm, 1)
                pe.wait_ge(s_rest, after(p - 1))
                settle(pe)
                for c_ in range(DC):
                    m = nc.tensor.matmul(bc_ps[0:2 * N, :], K.w_bc[:, c_, :], K.xt[:, c_, cols],
                                         start=(c_ == 0), stop=(c_ == DC - 1))
                m.then_inc(bc_mm, 1)
                if pair_exists(p + 1):
                    turn(p + 1, 1 - u)
                pe.wait_ge(low_ok, after(p))
                pe.wait_ge(z_ok, after(p - 1))
                for c_ in range(DC):
                    m = nc.tensor.matmul(z_ps[:, c_, :], K.w_dt[:, c_ * P:(c_ + 1) * P], low[:, :],
                                         start=True, stop=True)
                m.then_inc(z_mm, 1)

            turn(0, 0)
            over_pairs(pe, pair)


def scan_states(K):
    nc, sem = K.nc, K.sem
    S = N * DC
    RING = 4
    AHEAD = 8
    with ExitStack() as c:
        sb = lambda name, shape, dt=F32: c.enter_context(nc.sbuf_tensor(name, shape, dt))
        ps = lambda name, shape: c.enter_context(nc.psum_tensor(name, shape, F32))
        b_sb = [sb(f"sc_b{i}", [P, PT]) for i in range(RING)]
        u_sb = [sb(f"sc_u{i}", [P, PT]) for i in range(RING)]
        h_sb = [sb(f"sc_h{i}", [P, PT]) for i in range(RING)]
        hc_sb = [sb(f"sc_hc{i}", [P, PT]) for i in range(RING)]
        y_ps = ps("sc_y", [P, DC, PT])
        da_ps = [ps(f"sc_da{i}", [P, PT]) for i in range(2)]
        b_ps = [ps(f"sc_bps{i}", [P, PT]) for i in range(2)]
        c_ps = [ps(f"sc_cps{i}", [P, PT]) for i in range(2)]
        da0 = sem("sc_da0")
        spread = sem("sc_spread")
        spread_cs = sem("sc_spread_cs")
        da_ok = sem("sc_da_ok")
        y_out = sem("sc_y_out")
        b_ok = sem("sc_b_ok")
        u_ok = sem("sc_u_ok")
        h_ok = sem("sc_h_ok")
        hc_ok = sem("sc_hc_ok")
        summed = sem("sc_summed")
        block = c.enter_context(nc.Block())

        def done(p, s, ago=0, unit=S):
            return p * unit + (AHEAD + s - ago + 1)

        @block.scalar
        def _(act):
            act.sem_inc(b_ok, AHEAD)
            act.wait_ge(da0, 2)

            def copy_b(p, n):
                act.wait_ge(spread, p * N + n + 1)
                act.wait_ge(u_ok, done(p, n * DC + 1, RING * DC))
                nc.scalar.activation(b_sb[n % RING][:, :], b_ps[n % 2][:, :], ACT.Copy).then_inc(b_ok, 1)

            def pair(p, last):
                for n in range(N):
                    if not last or n + 1 < N:
                        copy_b(p, n + 1)
                    for dh in range(DC):
                        s = n * DC + dh
                        act.wait_ge(h_ok, done(p, s, 2))
                        settle(act)
                        cols = bass.ds(p * PT, PT)
                        o = da_ps[dh][:, :].rearrange("p (b l) -> p b l", b=2)[:, :, 1:L]
                        i = K.delta[:, dh, cols].rearrange("p (b l) -> p b l", b=2)[:, :, 1:L]
                        nc.scalar.activation(o, i, ACT.Exp, scale=K.a_neg[:, dh, n:n + 1]).then_inc(da_ok, 1)

            copy_b(0, 0)
            with act.Fori(0, NP - 1) as p:
                pair(p, False)
            pair(NP - 1, True)

        @block.gpsimd
        def _(pool):
            pool.sem_inc(u_ok, AHEAD)
            with pool.Fori(0, NP) as p:
                for n in range(N):
                    for dh in range(DC):
                        s = n * DC + dh
                        pool.wait_ge(b_ok, done(p, n, unit=N))
                        pool.wait_ge(h_ok, done(p, s, RING))
                        settle(pool)
                        nc.gpsimd.tensor_tensor(u_sb[s % RING][:, :], K.dx[:, dh, bass.ds(p * PT, PT)],
                                                b_sb[n % RING][:, :], ALU.mult).then_inc(u_ok, 1)

        @block.vector
        def _(dve):
            for i in range(2):
                nc.vector.memset(da_ps[i][:, :], 0.0).then_inc(da0, 1)
            dve.sem_inc(h_ok, AHEAD)
            dve.sem_inc(hc_ok, AHEAD)
            dve.sem_inc(y_out, DC)

            def scan(p, s):
                dve.wait_ge(da_ok, p * S + s + 1)
                dve.wait_ge(u_ok, done(p, s))
                dve.wait_ge(hc_ok, done(p, s, RING))
                nc.vector.tensor_tensor_scan(h_sb[s % RING][:, :], da_ps[s % 2][:, :], u_sb[s % RING][:, :], 0.0,
                                             ALU.mult, ALU.add).then_inc(h_ok, 1)

            def times_c(p, s):
                dve.wait_ge(h_ok, done(p, s))
                dve.wait_ge(summed, done(p, s, RING))
                dve.wait_ge(spread_cs, p * N + s // DC + 1)
                nc.vector.tensor_tensor(hc_sb[s % RING][:, :], h_sb[s % RING][:, :], c_ps[(s // DC) % 2][:, :],
                                        ALU.mult).then_inc(hc_ok, 1)

            def pair(p, last):
                for n in range(N):
                    if n + 1 < N:
                        for dh in range(DC):
                            scan(p, (n + 1) * DC + dh)
                    for dh in range(DC):
                        times_c(p, n * DC + dh)
                if not last:
                    for dh in range(DC):
                        scan(p + 1, dh)
                dve.wait_ge(summed, done(p, S - 1))
                for dh in range(DC):
                    cols = bass.ds(p * PT, PT)
                    nc.vector.scalar_tensor_tensor(out=K.delta[:, dh, cols], in0=K.xt[:, dh, cols],
                                                   scalar=K.d_skip[:, dh:dh + 1], in1=y_ps[:, dh, :],
                                                   op0=ALU.mult, op1=ALU.add).then_inc(y_out, 1)

            for dh in range(DC):
                scan(0, dh)
            with dve.Fori(0, NP - 1) as p:
                pair(p, False)
            pair(NP - 1, True)

        @block.tensor
        def _(pe):
            pe.sem_inc(summed, AHEAD)

            def spread_b(p, n):
                pe.wait_ge(b_ok, done(p, n, 2, N))
                nc.tensor.matmul(b_ps[n % 2][:, :], K.bc_sel[:, n % N, :], K.bc3[:, bass.ds((p + n // N) * PT, PT)],
                                 start=True, stop=True).then_inc(spread, 1)

            def spread_c(p, n):
                nc.tensor.matmul(c_ps[n % 2][:, :], K.bc_sel[:, N + n % N, :],
                                 K.bc3[:, bass.ds((p + n // N) * PT, PT)], start=True,
                                 stop=True).then_inc(spread_cs, 1)

            def pair(p, last):
                for n in range(N):
                    if not last or n + 4 < N:
                        spread_b(p, n + 4)
                    pe.wait_ge(hc_ok, done(p, n * DC + 1))
                    if not last or n + 2 < N:
                        spread_c(p, n + 2)
                    if n == 0:
                        pe.wait_ge(y_out, p * DC + DC)
                    for dh in range(DC):
                        s = n * DC + dh
                        nc.tensor.matmul(y_ps[:, dh, :], K.ident[:, :], hc_sb[s % RING][:, :], start=(n == 0),
                                         stop=(n == N - 1)).then_inc(summed, 1)

            for n in range(2):
                spread_b(0, n)
                spread_c(0, n)
            spread_b(0, 2)
            spread_b(0, 3)
            with pe.Fori(0, NP - 1) as p:
                pair(p, False)
            pair(NP - 1, True)


def distances(K):
    nc, sem = K.nc, K.sem
    with ExitStack() as c:
        sb = lambda name, shape, dt=F32: c.enter_context(nc.sbuf_tensor(name, shape, dt))
        ps = lambda name, shape: c.enter_context(nc.psum_tensor(name, shape, F32))
        old = K.xt[:, :, :].rearrange("p c t -> p (c t)")
        slot = lambda i: old[:, i * PTT * D:(i + 1) * PTT * D]
        cx = [slot(u).rearrange("p (t d) -> p t d", t=PTT) for u in range(2)]
        yt = [slot(2 + u).rearrange("p (c t) -> p c t", c=DC) for u in range(2)]
        s_sb = [slot(4 + u).rearrange("p (t d) -> p t d", t=PTT) for u in range(2)]
        st_sb = [slot(6 + u).rearrange("p (c t) -> p c t", c=DC) for u in range(2)]
        sq = [sb(f"di_sq{u}", [P, DC, PT]) for u in range(2)]
        ct_sb = [sb(f"di_ct{u}", [P, DC, PT]) for u in range(2)]
        dd = [sb(f"di_dd{u}", [P, PTT, L]) for u in range(2)]
        aa = [sb(f"di_aa{u}", [P, PTT]) for u in range(2)]
        junk = [sb(f"di_junk{u}", [P, PTT, D]) for u in range(2)]
        ones = sb("di_ones", [P, P])
        stats = sb("di_stats", [P, PTT, 6])
        mv = sb("di_mv", [P, PTT, 2])
        var = sb("di_var", [P, PTT])
        rstd = [sb(f"di_rstd{u}", [P, PTT]) for u in range(2)]
        nmr = [sb(f"di_nmr{u}", [P, PTT]) for u in range(2)]
        y_ps = ps("di_y", [P, PTT, D])
        st_ps = ps("di_st_ps", [P, DC, PT])
        ct_ps = ps("di_ct_ps", [P, DC, PT])
        d_ps = ps("di_d_ps", [P, PTT, L])

        set_up = sem("di_set_up")
        ctx_in = [sem(f"di_ctx_in{u}") for u in range(2)]
        yt_ok, y_tr, x_ok, s_ok = (sem("di_" + x) for x in ("yt_ok", "y_tr", "x_ok", "s_ok"))
        st_tr, st_ok, sq_ok = sem("di_st_tr"), sem("di_st_ok"), sem("di_sq_ok")
        ct_tr, ct_ok, aa_ok = sem("di_ct_tr"), sem("di_ct_ok"), sem("di_aa_ok")
        d_mm, d_ok, root = sem("di_d_mm"), sem("di_d_ok"), sem("di_root")
        SS = 9
        stt = sem("di_stats_ok")
        stored = [sem(f"di_stored{u}") for u in range(2)]
        K.wave_in = sem("wave_in")
        block = c.enter_context(nc.Block())
        x_rows = lambda p: K.x[:, bass.ds(p * PTT, PTT), :]

        @block.sync
        def _(sp):
            def load_ctx(p):
                sp.wait_ge(ct_tr, after(p - 2))
                sp.wait_ge(aa_ok, after(p - 2))
                sp.dma_start(cx[p % 2], K.ctx_dram[2 * p:2 * p + 2, :, :].rearrange("b (h p) d -> p (b h) d", p=P)
                             ).then_inc(ctx_in[p % 2], 16)

            load_ctx(0)
            load_ctx(1)
            sp.wait_ge(set_up, 2)
            for p in range(NP):
                if p + 2 < NP:
                    load_ctx(p + 2)
                sp.wait_ge(stored[p % 2], p // 2 * 16 + 32)
                for s in range(SEG):
                    sp.dma_start(K.wave[s * B + 2 * p:s * B + 2 * p + 2, s * LAG * SW:(s * LAG + L) * SW].rearrange(
                                     "b (i j) -> b i j", j=SW),
                                 K.dist_dram[2 * p:2 * p + 2, :, s * SW:(s + 1) * SW]).then_inc(K.wave_in, 16)
            sp.wait_ge(K.wave_in, 16 * SEG * NP)

        @block.gpsimd
        def _(pool):
            start(pool, yt_ok)

            def pair(q, u):
                p = q * 2 + u
                pool.wait_ge(y_tr, after(p - 2))
                settle(pool)
                nc.gpsimd.tensor_copy(yt[u], K.delta[:, :, bass.ds(p * PT, PT)]).then_inc(yt_ok, 1)

            pair(0, 0)
            pair(0, 1)
            nc.gpsimd.memset(ones[:, :], 1.0).then_inc(set_up, 1)
            nc.gpsimd.memset(K.wave[:, :], 0.0).then_inc(set_up, 1)
            with pool.Fori(1, NP // 2) as q:
                for u in range(2):
                    pair(q, u)

        @block.vector
        def _(dve):
            start(dve, x_ok, ct_ok)

            def pair(q, u):
                p = q * 2 + u
                dve.wait_ge(y_tr, after(p))
                settle(dve)
                nc.vector.tensor_tensor(x_rows(p), x_rows(p), y_ps[:, :, :], ALU.add).then_inc(x_ok, 1)
                dve.wait_ge(x_ok, after(p))
                tile_stats(dve, nc, stt, p * SS, [K.x[:, bass.ds(p * PTT + t, 1), :].rearrange("p a d -> p (a d)")
                                                  for t in range(PTT)], stats, mv)
                dve.wait_ge(stt, p * SS + 2)
                nc.vector.tensor_scalar(var[:, :], mv[:, :, 1], EPS, None, ALU.add).then_inc(stt, 1)
                dve.wait_ge(root, after(p))
                dve.wait_ge(s_ok, after(p - 2))
                refined_scales(dve, nc, stt, p * SS + 3, mv, var, rstd[u], nmr[u])
                dve.wait_ge(ct_tr, after(p))
                dve.wait_ge(d_mm, after(p - 2))
                nc.vector.tensor_scalar(ct_sb[u][:, :, :], ct_ps[:, :, :], -2.0, None, ALU.mult).then_inc(ct_ok, 1)

            over_pairs(dve, pair)

        @block.scalar
        def _(act):
            start(act, aa_ok, root, s_ok, st_ok, sq_ok, d_ok)
            for u in range(2):
                act.sem_inc(stored[u], 16)

            def normalized(q, u):
                p = q * 2 + u
                act.wait_ge(stt, p * SS + 3)
                nc.scalar.activation(mv[:, :, 1], var[:, :], ACT.Sqrt).then_inc(root, 1)
                act.wait_ge(ctx_in[u], q * 16 + 16)
                act.wait_ge(d_ok, after(p - 2))
                for t in range(PTT):
                    m = nc.scalar.activation(junk[u][:, t, :], cx[u][:, t, :], ACT.Square, accum_out=aa[u][:, t:t + 1])
                m.then_inc(aa_ok, 1)
                act.wait_ge(stt, p * SS + SS)
                act.wait_ge(st_tr, after(p - 2))
                settle(act)
                for t in range(PTT):
                    m = nc.scalar.activation(s_sb[u][:, t, :],
                                             K.x[:, bass.ds(p * PTT + t, 1), :].rearrange("p a d -> p (a d)"),
                                             ACT.Identity, bias=nmr[u][:, t:t + 1], scale=rstd[u][:, t:t + 1])
                m.then_inc(s_ok, 1)

            def pair(q, u):
                p = q * 2 + u
                act.wait_ge(st_tr, after(p))
                act.wait_ge(d_mm, after(p - 2))
                nc.scalar.activation(st_sb[u], st_ps[:, :, :], ACT.Copy).then_inc(st_ok, 1)
                act.wait_ge(st_ok, after(p))
                nc.scalar.activation(sq[u][:, :, :], st_sb[u], ACT.Square).then_inc(sq_ok, 1)
                if pair_exists(p + 1):
                    normalized(q + u, 1 - u)
                act.wait_ge(d_mm, after(p))
                act.wait_ge(stored[u], q * 16 + 16)
                for t in range(PTT):
                    m = nc.scalar.activation(dd[u][:, t, :], d_ps[:, t, :], ACT.Relu, bias=aa[u][:, t:t + 1])
                m.then_inc(d_ok, 1)
                act.wait_ge(d_ok, after(p))
                settle(act)
                act.dma_start(K.dist_dram[bass.ds(p * 2, 2), :, :].rearrange("b (h p) d -> p (b h) d", p=P),
                              dd[u][:, :, :]).then_inc(stored[u], 16)

            normalized(0, 0)
            over_pairs(act, pair)

        @block.tensor
        def _(pe):
            start(pe, y_tr, ct_tr, st_tr, d_mm)

            def turn(src, dst, done):
                for t in range(PTT):
                    for c_ in range(DC):
                        m = nc.tensor.transpose(dst[:, c_, t * P:(t + 1) * P], src[:, t, c_ * P:(c_ + 1) * P],
                                                K.ident[:, :])
                m.then_inc(done, 1)

            def inputs(q, u):
                p = q * 2 + u
                pe.wait_ge(yt_ok, after(p))
                pe.wait_ge(x_ok, after(p - 1))
                for t in range(PTT):
                    for c_ in range(DC):
                        m = nc.tensor.transpose(y_ps[:, t, c_ * P:(c_ + 1) * P], yt[u][:, c_, t * P:(t + 1) * P],
                                                K.ident[:, :])
                m.then_inc(y_tr, 1)
                pe.wait_ge(ctx_in[u], q * 16 + 16)
                pe.wait_ge(ct_ok, after(p - 1))
                turn(cx[u], ct_ps, ct_tr)

            def pair(q, u):
                p = q * 2 + u
                pe.wait_ge(s_ok, after(p))
                pe.wait_ge(st_ok, after(p - 1))
                turn(s_sb[u], st_ps, st_tr)
                if pair_exists(p + 1):
                    inputs(q + u, 1 - u)
                pe.wait_ge(sq_ok, after(p))
                pe.wait_ge(ct_ok, after(p))
                pe.wait_ge(d_ok, after(p - 1))
                for t in range(PTT):
                    j = slice(t // 2 * L, (t // 2 + 1) * L)
                    for c_ in range(DC):
                        nc.tensor.matmul(d_ps[:, t, :], ct_sb[u][:, c_, t * P:(t + 1) * P], st_sb[u][:, c_, j],
                                         start=(c_ == 0), stop=False)
                    for c_ in range(DC):
                        m = nc.tensor.matmul(d_ps[:, t, :], ones[:, :], sq[u][:, c_, j], start=False,
                                             stop=(c_ == DC - 1))
                m.then_inc(d_mm, 1)

            inputs(0, 0)
            pe.wait_ge(set_up, 1)
            over_pairs(pe, pair)


def wave(K):
    nc, sem = K.nc, K.sem
    with ExitStack() as c:
        sb = lambda name, shape, dt=F32: c.enter_context(nc.sbuf_tensor(name, shape, dt))
        r = sb("wv_r", [P, STEPS + 1 + LAG, SW + 1])
        MR = 4
        ROOTS = 8
        m_sb = [sb(f"wv_m{i}", [P, SW]) for i in range(MR)]
        code = sb("wv_code", [P, STEPS, 2, SW], F16)
        shift = sb("wv_shift", [P, P])
        edge_big = sb("wv_edge_big", [P, 1])
        first = sb("wv_first", [P, 1])
        e_ps = [c.enter_context(nc.psum_tensor(f"wv_e{i}", [P, 512], F32)) for i in range(4)]
        set_up = sem("wv_set_up")
        mats = sem("wv_mats")
        roots = sem("wv_roots")
        m_ok = sem("wv_m_ok")
        r_ok = sem("wv_r_ok")
        e_mm = sem("wv_e_mm")
        edge_ok = sem("wv_edge_ok")
        code_ok = sem("wv_code_ok")
        K.code_in = sem("code_in")
        block = c.enter_context(nc.Block())

        @block.gpsimd
        def _(pool):
            nc.gpsimd.memset(shift[:, :], 0.0).then_inc(mats, 1)
            nc.gpsimd.memset(edge_big[:, :], 0.0).then_inc(mats, 1)
            nc.gpsimd.memset(first[:, :], BIG).then_inc(mats, 1)
            pool.wait_ge(mats, 3)
            nc.gpsimd.affine_select(out=shift[:, :], in_=shift[:, :], compare_op=ALU.not_equal, fill=1.0, base=B,
                                    pattern=[[-1, P]], channel_multiplier=1).then_inc(set_up, 1)
            nc.gpsimd.memset(edge_big[0:B, :], BIG).then_inc(set_up, 1)
            nc.gpsimd.memset(first[0:B, :], 0.0).then_inc(set_up, 1)

        @block.sync
        def _(sp):
            for k in range(BLK):
                for s in range(SEG):
                    t0 = k * BR + s * LAG
                    sp.wait_ge(code_ok, 2 * (t0 + BR))
                    sp.dma_start(K.codes[k * B:(k + 1) * B, s, :, :, :].rearrange("p i a j -> p (i a j)"),
                                 code[s * B:(s + 1) * B, t0:t0 + BR, :, :].rearrange("p i a j -> p (i a j)")
                                 ).then_inc(K.code_in, 16)
            sp.wait_ge(K.code_in, 16 * BLK * SEG)

        @block.vector
        def _(dve):
            nc.vector.memset(r[:, 0, :], BIG).then_inc(m_ok, 1)
            nc.vector.memset(r[:, 1:LAG + 1, 0:1], BIG).then_inc(edge_ok, LAG)
            dve.wait_ge(set_up, 3)
            dve.wait_ge(m_ok, 1)

            def code_left(t):
                nc.vector.tensor_tensor(code[:, t, 0, :], r[:, t + 1, 0:SW], m_sb[t % MR][:, :],
                                        ALU.is_lt).then_inc(code_ok, 1)

            def code_up(t):
                nc.vector.tensor_tensor(code[:, t, 1, :], r[:, t, 1:SW + 1], r[:, t, 0:SW],
                                        ALU.is_lt).then_inc(code_ok, 1)

            for t in range(STEPS):
                if t % ROOTS == 0:
                    dve.wait_ge(roots, t // ROOTS + 1)
                dve.wait_ge(edge_ok, t + 1)
                if t:
                    dve.wait_ge(r_ok, t)
                nc.vector.tensor_tensor(m_sb[t % MR][:, :], r[:, t, 0:SW], r[:, t, 1:SW + 1], ALU.min
                                        ).then_inc(m_ok, 1)
                if t:
                    code_left(t - 1)
                dve.wait_ge(m_ok, t + 2)
                first_left = first[:, :] if t == 0 else r[:, t + 1, 0:1]
                nc.vector.tensor_tensor_scan(r[:, t + 1, 1:SW + 1], m_sb[t % MR][:, :],
                                             K.wave[:, t * SW:(t + 1) * SW], first_left, ALU.min,
                                             ALU.add).then_inc(r_ok, 1)
                code_up(t)
            dve.wait_ge(r_ok, STEPS)
            code_left(STEPS - 1)

        @block.scalar
        def _(act):
            def root(n):
                cols = slice(n * ROOTS * SW, min((n + 1) * ROOTS, STEPS) * SW)
                nc.scalar.activation(K.wave[:, cols], K.wave[:, cols], ACT.Sqrt).then_inc(roots, 1)

            root(0)
            root(1)
            act.wait_ge(set_up, 3)
            for t in range(STEPS):
                if t % ROOTS == 0 and t + 2 * ROOTS < STEPS:
                    root(t // ROOTS + 2)
                act.wait_ge(e_mm, t + 1)
                nc.scalar.activation(r[:, t + LAG + 1, 0:1], e_ps[t % 4][:, 0:1], ACT.Identity,
                                     bias=edge_big[:, :]).then_inc(edge_ok, 1)

        @block.tensor
        def _(pe):
            pe.wait_ge(set_up, 3)
            for t in range(STEPS):
                pe.wait_ge(edge_ok, t + 1)
                pe.wait_ge(r_ok, t + 1)
                nc.tensor.matmul(e_ps[t % 4][:, 0:1], shift[:, :], r[:, t + 1, SW:SW + 1], start=True,
                                 stop=True).then_inc(e_mm, 1)


def trace_back(K):
    nc, sem = K.nc, K.sem
    MARK = 600.0
    with ExitStack() as c:
        sb = lambda name, shape, dt=F32: c.enter_context(nc.sbuf_tensor(name, shape, dt))
        left = sb("tb_left", [P, BR, L], F16)
        up = sb("tb_up", [P, BR, L], F16)
        dg = sb("tb_dg", [P, BR, L], F16)
        t1 = sb("tb_t1", [P, BR, L], F16)
        exits = sb("tb_exits", [P, BR, L], F16)
        col = sb("tb_col", [P, L], F16)
        col_m = sb("tb_col_m", [P, L], F16)
        maps = [sb(f"tb_map{i}", [P, 2 + L], F16) for i in range(2)]
        cand = [sb(f"tb_cand{i}", [P, L], F16) for i in range(3)]
        junk = [sb(f"tb_junk{i}", [P, L], F16) for i in range(2)]
        entry0 = sb("tb_entry0", [P, 1])
        entry = sb("tb_entry", [P, 1])
        found = sb("tb_found", [P, 1])
        hi = sb("tb_hi", [P, 1 + BR])
        ex = sb("tb_ex", [P, BR])
        off = sb("tb_off", [P, BR])
        lo = sb("tb_lo", [P, BR])
        shift = sb("tb_shift", [P, P])
        s_ps = c.enter_context(nc.psum_tensor("tb_s", [P, 512], F32))
        hi_ps = c.enter_context(nc.psum_tensor("tb_hi_ps", [P, 512], F32))
        lo_ps = c.enter_context(nc.psum_tensor("tb_lo_ps", [P, 512], F32))
        raw, set_up = sem("tb_raw"), sem("tb_set_up")
        cx_in = sem("tb_cx_in")
        st = sem("tb_steps")
        gathered = sem("tb_gathered")
        shifted = sem("tb_shifted")
        turned = sem("tb_turned")
        spread = sem("tb_spread")
        block = c.enter_context(nc.Block())

        @block.sync
        def _(sp):
            sp.wait_ge(st, 2)
            for p in range(NP):
                sp.dma_start(K.cx[:, p * PTT:(p + 1) * PTT, :],
                             K.ctx_dram[2 * p:2 * p + 2, :, :].rearrange("b (h p) d -> p (b h) d", p=P)
                             ).then_inc(cx_in, 16)
            sp.wait_ge(cx_in, 16 * NP)

        @block.gpsimd
        def _(pool):
            nc.gpsimd.memset(shift[:, :], 0.0).then_inc(raw, 1)
            nc.gpsimd.memset(entry0[:, :], float(L - 1)).then_inc(raw, 1)
            pool.wait_ge(raw, 2)
            nc.gpsimd.affine_select(out=shift[:, :], in_=shift[:, :], compare_op=ALU.not_equal, fill=1.0, base=-B,
                                    pattern=[[-1, P]], channel_multiplier=1).then_inc(set_up, 1)
            nc.gpsimd.affine_select(out=entry0[:, :], in_=entry0[:, :], compare_op=ALU.is_ge, fill=0.0,
                                    base=-B * (BLK - 1), pattern=[[0, 1]], channel_multiplier=1).then_inc(set_up, 1)
            nc.gpsimd.iota(col[:, :], [[1, L]], base=0, channel_multiplier=0,
                           allow_small_or_imprecise_dtypes=True).then_inc(set_up, 1)
            nc.gpsimd.iota(col_m[:, :], [[1, L]], base=int(MARK), channel_multiplier=0,
                           allow_small_or_imprecise_dtypes=True).then_inc(set_up, 1)
            nc.gpsimd.iota(maps[1][:, :], [[1, L + 2]], base=-2, channel_multiplier=0,
                           allow_small_or_imprecise_dtypes=True).then_inc(set_up, 1)
            nc.gpsimd.memset(maps[0][:, 0:2], 0.0).then_inc(set_up, 1)

        @block.vector
        def _(dve):
            n = [0]

            def did(ins):
                n[0] += 1
                ins.then_inc(st, 1)
                return n[0]

            view = lambda a: K.codes[:, :, :, a, :].rearrange("p s i j -> p i s j")
            to = lambda x: x[:, :, :].rearrange("p i (s j) -> p i s j", j=SW)
            dve.wait_ge(set_up, 6)
            a = did(nc.vector.tensor_copy(to(left), view(0)))
            did(nc.vector.tensor_tensor(to(up), view(1), view(0), ALU.is_gt))
            dve.wait_ge(st, n[0])
            did(nc.vector.tensor_tensor(t1[:, :, :], left[:, :, :], up[:, :, :], ALU.add))
            dve.wait_ge(st, n[0])
            did(nc.vector.tensor_scalar(dg[:, :, :], t1[:, :, :], -1.0, 1.0, ALU.mult, ALU.add))
            dve.wait_ge(st, n[0])

            bc = lambda x: x[:, :].rearrange("p (a j) -> p a j", a=1).broadcast_to([P, BR, L])
            did(nc.vector.tensor_tensor(t1[:, :, :], up[:, :, :], bc(col), ALU.mult))
            did(nc.vector.tensor_tensor(exits[:, :, :], dg[:, :, :], bc(col_m), ALU.mult))
            dve.wait_ge(st, n[0])
            did(nc.vector.tensor_tensor(t1[:, :, :], t1[:, :, :], exits[:, :, :], ALU.add))
            dve.wait_ge(st, n[0])
            flat = lambda x: x[:, :, :].rearrange("p i j -> p (i j)")
            did(nc.vector.tensor_tensor_scan(flat(exits), flat(left), flat(t1), 0.0, ALU.mult, ALU.add))

            for i in range(BR):
                old, new = maps[(i + 1) % 2], maps[i % 2]
                did(nc.vector.tensor_tensor(cand[0][:, :], up[:, i, :], old[:, 2:2 + L], ALU.mult))
                did(nc.vector.tensor_tensor(cand[1][:, :], dg[:, i, :], old[:, 1:1 + L], ALU.mult))
                dve.wait_ge(st, n[0])
                did(nc.vector.tensor_tensor(cand[2][:, :], cand[0][:, :], cand[1][:, :], ALU.add))
                dve.wait_ge(st, n[0])
                did(nc.vector.tensor_tensor_scan(new[:, 2:2 + L], left[:, i, :], cand[2][:, :], 0.0, ALU.mult,
                                                 ALU.add))
                dve.wait_ge(st, n[0])
            last = maps[(BR - 1) % 2]

            did(nc.vector.tensor_copy(entry[:, :], entry0[:, :]))
            for k in range(BLK - 1):
                dve.wait_ge(st, n[0])
                nc.vector.scalar_tensor_tensor(out=junk[0][:, :], in0=col[:, :], scalar=entry[:, :],
                                               in1=last[:, 2:2 + L], op0=ALU.is_equal, op1=ALU.mult,
                                               accum_out=found[:, :]).then_inc(gathered, 1)
                dve.wait_ge(shifted, k + 1)
                did(nc.vector.tensor_tensor(entry[:, :], s_ps[:, 0:1], entry0[:, :], ALU.add))
            dve.wait_ge(st, n[0])
            did(nc.vector.tensor_copy(hi[:, BR:BR + 1], entry[:, :]))

            for i in reversed(range(BR)):
                dve.wait_ge(st, n[0])
                did(nc.vector.scalar_tensor_tensor(out=junk[i % 2][:, :], in0=col[:, :], scalar=hi[:, 1 + i:2 + i],
                                                   in1=exits[:, i, :], op0=ALU.is_equal, op1=ALU.mult,
                                                   accum_out=ex[:, i:i + 1]))
                dve.wait_ge(st, n[0])
                did(nc.vector.tensor_scalar(off[:, i:i + 1], ex[:, i:i + 1], MARK, -(MARK + 1), ALU.is_ge, ALU.mult))
                dve.wait_ge(st, n[0])
                did(nc.vector.tensor_tensor(hi[:, i:i + 1], ex[:, i:i + 1], off[:, i:i + 1], ALU.add))
            dve.wait_ge(st, n[0])
            nc.vector.scalar_tensor_tensor(out=lo[:, :], in0=ex[:, :], scalar=MARK, in1=hi[:, 0:BR], op0=ALU.is_ge,
                                           op1=ALU.add).then_inc(gathered, 1)

            dve.wait_ge(turned, 2)
            for k in range(BLK):
                q, h = k % (P // BR), k // (P // BR)
                m = nc.vector.tensor_copy(K.hi[q * BR:(q + 1) * BR, h, :], hi_ps[0:BR, k * B:(k + 1) * B])
                m = nc.vector.tensor_copy(K.lo[q * BR:(q + 1) * BR, h, :], lo_ps[0:BR, k * B:(k + 1) * B])
            m.then_inc(spread, 1)

        @block.tensor
        def _(pe):
            pe.wait_ge(set_up, 1)
            for k in range(BLK - 1):
                pe.wait_ge(gathered, k + 1)
                nc.tensor.matmul(s_ps[:, 0:1], shift[:, :], found[:, :], start=True, stop=True).then_inc(shifted, 1)
            pe.wait_ge(gathered, BLK)
            nc.tensor.transpose(hi_ps[0:BR, 0:P], hi[:, 1:1 + BR], K.ident[:, :]).then_inc(turned, 1)
            nc.tensor.transpose(lo_ps[0:BR, 0:P], lo[:, :], K.ident[:, :]).then_inc(turned, 1)


def expand(K):
    nc, sem = K.nc, K.sem
    with ExitStack() as c:
        sb = lambda name, shape, dt=F32: c.enter_context(nc.sbuf_tensor(name, shape, dt))
        ps = lambda name, shape: c.enter_context(nc.psum_tensor(name, shape, F32))
        col = sb("ex_col", [P, L])
        upto = [sb(f"ex_upto{u}", [P, 2, L]) for u in range(2)]
        on = [sb(f"ex_on{u}", [P, 2, L]) for u in range(2)]
        stats = sb("ex_stats", [P, TT, 6])
        mv = sb("ex_mv", [P, TT, 2])
        var = sb("ex_var", [P, TT])
        rstd = sb("ex_rstd", [P, TT])
        nmr = sb("ex_nmr", [P, TT])
        xn = [sb(f"ex_xn{u}", [P, 2, D]) for u in range(4)]
        xt = [sb(f"ex_xt{u}", [P, DC, L]) for u in range(2)]
        logits = [sb(f"ex_logits{u}", [P, 2, E]) for u in range(2)]
        most = [sb(f"ex_most{u}", [P, 2, 8]) for u in range(2)]
        most_at = [sb(f"ex_most_at{u}", [P, 2, 8], U32) for u in range(2)]
        e_ps = [ps(f"ex_e{u}", [P, 2, D]) for u in range(2)]
        xt_ps = [ps(f"ex_xt_ps{u}", [P, DC, L]) for u in range(2)]
        l_ps = [ps(f"ex_l{u}", [P, 4, P]) for u in range(2)]

        col_ok = sem("ex_col_ok")
        half = sem("ex_half")
        mask = sem("ex_mask")
        e_mm, x_ok = sem("ex_e_mm"), sem("ex_x_ok")
        part = sem("ex_part")
        stt = sem("ex_stats_ok")
        root = sem("ex_root")
        xn_ok, t_ok, xt_ok, l_mm, l_ok = (sem("ex_" + x) for x in ("xn_ok", "t_ok", "xt_ok", "l_mm", "l_ok"))
        top = sem("ex_top")
        kept = sem("ex_kept")
        xn_out = [sem(f"ex_xn_out{u}") for u in range(4)]
        block = c.enter_context(nc.Block())
        tile = lambda buf, t: buf[:, bass.ds(t, 1), :].rearrange("p a d -> p (a d)")

        @block.sync
        def _(sp):
            for u in range(4):
                sp.sem_inc(xn_out[u], 16)
            for r in range(WRING):
                load_weights(K, sp, r, r)
            with sp.Fori(0, B // 4) as q:
                for u in range(4):
                    b = q * 4 + u
                    sp.wait_ge(xn_ok, after(b))
                    settle(sp)
                    sp.dma_start(K.xn_dram[bass.ds(b * L, L), :].rearrange("(t p) d -> p t d", p=P),
                                 xn[u][:, :, :]).then_inc(xn_out[u], 16)
            for u in range(4):
                sp.wait_ge(xn_out[u], 16 * (B // 4) + 16)

        @block.gpsimd
        def _(pool):
            nc.gpsimd.iota(col[:, :], [[1, L]], base=0, channel_multiplier=0,
                           allow_small_or_imprecise_dtypes=True).then_inc(col_ok, 1)

        @block.vector
        def _(dve):
            start(dve, x_ok, xt_ok, kept)
            dve.wait_ge(col_ok, 1)

            def masks(b, u):
                dve.wait_ge(e_mm, after(b - 2))
                settle(dve)
                for h in range(2):
                    nc.vector.tensor_scalar(upto[u][:, h, :], col[:, :], K.hi[:, h, bass.ds(b, 1)], None,
                                            ALU.is_le).then_inc(half, 1)
                dve.wait_ge(half, b * 2 + 2)
                settle(dve)
                for h in range(2):
                    m = nc.vector.scalar_tensor_tensor(out=on[u][:, h, :], in0=col[:, :],
                                                       scalar=K.lo[:, h, bass.ds(b, 1)], in1=upto[u][:, h, :],
                                                       op0=ALU.is_ge, op1=ALU.mult)
                m.then_inc(mask, 1)

            def add(b, u):
                rows = K.x[:, bass.ds(b * 2, 2), :]
                dve.wait_ge(e_mm, after(b))
                settle(dve)
                nc.vector.tensor_tensor(rows, rows, e_ps[u][:, :, :], ALU.add).then_inc(x_ok, 1)
                dve.wait_ge(x_ok, after(b))
                settle(dve)
                for t in range(2):
                    m = nc.vector.bn_stats(tile(stats, b * 2 + t), tile(K.x, b * 2 + t))
                m.then_inc(part, 1)

            masks(0, 0)
            with dve.Fori(0, B // 2 - 1) as q:
                for u in range(2):
                    masks(q * 2 + u + 1, (u + 1) % 2)
                    add(q * 2 + u, u)
            masks(B - 1, 1)
            add(B - 2, 0)
            add(B - 1, 1)
            dve.wait_ge(part, B)
            for t in range(TT):
                m = nc.vector.bn_aggr(mv[:, t, :], stats[:, t, :])
            m.then_inc(stt, 1)
            dve.wait_ge(stt, 1)
            nc.vector.tensor_scalar(var[:, :], mv[:, :, 1], EPS, None, ALU.add).then_inc(stt, 1)
            dve.wait_ge(root, 1)
            refined_scales(dve, nc, stt, 2, mv, var, rstd, nmr)

            def take_turned(b, u):
                dve.wait_ge(t_ok, after(b))
                dve.wait_ge(l_mm, after(b - 2))
                nc.vector.tensor_copy(xt[u][:, :, :], xt_ps[u][:, :, :]).then_inc(xt_ok, 1)

            def batch(q, u4):
                b, u = q * 4 + u4, u4 % 2
                if batch_exists(b + 1):
                    take_turned(b + 1, 1 - u)
                dve.wait_ge(l_ok, after(b))
                settle(dve)
                for t in range(2):
                    m = nc.vector.max(most[u][:, t, :], logits[u][:, t, :])
                m.then_inc(top, 1)
                dve.wait_ge(top, b * 2 + 1)
                settle(dve)
                for t in range(2):
                    m = nc.vector.max_index(most_at[u][:, t, :], most[u][:, t, :], logits[u][:, t, :])
                m.then_inc(top, 1)
                dve.wait_ge(top, b * 2 + 2)
                settle(dve)
                by_choice = lambda x: x[:, :, 0:2].rearrange("p t i -> p i t")
                nc.vector.tensor_copy(K.top[:, :, bass.ds(b * 2, 2)], by_choice(most[u]))
                nc.vector.tensor_copy(K.top_at[:, :, bass.ds(b * 2, 2)], by_choice(most_at[u])).then_inc(kept, 1)

            take_turned(0, 0)
            over_batches(dve, batch)

        @block.scalar
        def _(act):
            act.wait_ge(stt, 2)
            nc.scalar.activation(mv[:, :, 1], var[:, :], ACT.Sqrt).then_inc(root, 1)
            act.wait_ge(stt, 8)

            def normalize(q, u4):
                b = q * 4 + u4
                act.wait_ge(t_ok, after(b - 2))
                act.wait_ge(xn_out[u4], q * 16 + 16)
                settle(act)
                for t in range(2):
                    m = nc.scalar.activation(xn[u4][:, t, :], tile(K.x, b * 2 + t), ACT.Identity,
                                             bias=nmr[:, bass.ds(b * 2 + t, 1)], scale=rstd[:, bass.ds(b * 2 + t, 1)])
                m.then_inc(xn_ok, 1)

            def batch(q, u4):
                b, u = q * 4 + u4, u4 % 2
                if batch_exists(b + 2):
                    normalize(q + (u4 + 2) // 4, (u4 + 2) % 4)
                act.wait_ge(l_mm, after(b))
                act.wait_ge(kept, after(b - 2))
                nc.scalar.activation(logits[u][:, :, :], l_ps[u][:, 0:2, 0:E], ACT.Copy).then_inc(l_ok, 1)

            start(act, xn_ok, l_ok)
            normalize(0, 0)
            normalize(0, 1)
            over_batches(act, batch)

        @block.tensor
        def _(pe):
            start(pe, e_mm, t_ok, l_mm)
            with pe.Fori(0, B // 2) as q:
                for u in range(2):
                    b = q * 2 + u
                    pe.wait_ge(mask, b + 1)
                    pe.wait_ge(x_ok, after(b - 2))
                    for j in range(2):
                        for h in range(2):
                            m = nc.tensor.matmul(e_ps[u][:, j, :], on[u][:, h, j * P:(j + 1) * P],
                                                 tile(K.cx, b * 2 + h), start=(h == 0), stop=(h == 1))
                    m.then_inc(e_mm, 1)

            def turn(b, u4):
                u = u4 % 2
                pe.wait_ge(xn_ok, after(b))
                pe.wait_ge(xt_ok, after(b - 2))
                for t in range(2):
                    for c_ in range(DC):
                        m = nc.tensor.transpose(xt_ps[u][:, c_, t * P:(t + 1) * P],
                                                xn[u4][:, t, c_ * P:(c_ + 1) * P], K.ident[:, :])
                m.then_inc(t_ok, 1)

            def batch(q, u4):
                b, u = q * 4 + u4, u4 % 2
                if batch_exists(b + 1):
                    turn(b + 1, (u4 + 1) % 4)
                pe.wait_ge(xt_ok, after(b))
                pe.wait_ge(l_ok, after(b - 2))
                for t in range(2):
                    for c_ in range(DC):
                        m = nc.tensor.matmul(l_ps[u][:, t, 0:E], xt[u][:, c_, t * P:(t + 1) * P],
                                             K.gate[:, c_, :], start=(c_ == 0), stop=(c_ == DC - 1))
                m.then_inc(l_mm, 1)

            turn(0, 0)
            over_batches(pe, batch)


def route(K):
    nc, sem = K.nc, K.sem
    with ExitStack() as c:
        sb = lambda name, shape, dt=F32: c.enter_context(nc.sbuf_tensor(name, shape, dt))
        ps = lambda name, shape: c.enter_context(nc.psum_tensor(name, shape, F32))
        expert = sb("ro_expert", [P, E])
        place = sb("ro_place", [P, MT + 1])
        token = sb("ro_token", [P, 2, TT])
        empty = sb("ro_empty", [P, 1])
        entry = sb("ro_entry", [P, 2 * TT])
        ones = sb("ro_ones", [P, P], BF16)
        later = sb("ro_later", [P, P], BF16)
        hot = [sb(f"ro_hot{i}", [P, E, TT]) for i in range(2)]
        chosen = sb("ro_chosen", [P, E, TT], BF16)
        going = sb("ro_going", [P, E, TT], BF16)
        upto = sb("ro_upto", [P, E, TT], BF16)
        picked = [sb(f"ro_picked{i}", [P, E, TT]) for i in range(2)]
        first = sb("ro_first", [P, E, TT])
        count = sb("ro_count", [P, E], I32)
        up = sb("ro_up", [P, E], I32)
        tiles = sb("ro_tiles", [P, E])
        one = sb("ro_one", [P, E])
        ends = sb("ro_ends", [P, E])
        start_at = sb("ro_start", [P, E])
        hi_i = sb("ro_hi_i", [P, 2, TT], I32)
        lo_i = sb("ro_lo_i", [P, 2, TT], I32)
        pos = sb("ro_pos", [P, 2, TT])
        pos_i = sb("ro_pos_i", [P, 2, TT], I32)
        hi = sb("ro_hi", [P, 2 * TT])
        lo = sb("ro_lo", [P, 2 * TT])
        gap = sb("ro_gap", [P, TT])
        ex = sb("ro_exp", [P, TT])
        ex1 = sb("ro_exp1", [P, TT])
        at_lo = [sb(f"ro_at_lo{i}", [P, P]) for i in range(4)]
        at_hi = [sb(f"ro_at_hi{i}", [P, MT + 1]) for i in range(4)]
        GE = E // 4
        rank_ps = [ps(f"ro_rank{g}", [P, GE, TT]) for g in range(4)]
        count_ps = ps("ro_count_ps", [P, 512])
        table_ps = ps("ro_table", [P, 512])
        set_up, raw = sem("ro_set_up"), sem("ro_raw")
        st = sem("ro_steps")
        sums = sem("ro_sums")
        exp_ok = sem("ro_exp_ok")
        gap_ok = sem("ro_gap_ok")
        ranks = sem("ro_ranks")
        marks = sem("ro_marks")
        used = sem("ro_used")
        tabled = sem("ro_tabled")
        block = c.enter_context(nc.Block())

        @block.gpsimd
        def _(pool):
            nc.gpsimd.memset(later[:, :], 0.0).then_inc(raw, 1)
            nc.gpsimd.memset(ones[:, :], 1.0).then_inc(set_up, 1)
            nc.gpsimd.memset(one[:, :], 1.0).then_inc(set_up, 1)
            nc.gpsimd.iota(expert[:, :], [[1, E]], base=0, channel_multiplier=0,
                           allow_small_or_imprecise_dtypes=True).then_inc(set_up, 1)
            nc.gpsimd.iota(place[:, :], [[1, MT + 1]], base=0, channel_multiplier=0,
                           allow_small_or_imprecise_dtypes=True).then_inc(set_up, 1)
            nc.gpsimd.iota(token[:, :, :], [[TOK, 2], [P, TT]], base=-2 * TOK, channel_multiplier=1,
                           allow_small_or_imprecise_dtypes=True).then_inc(set_up, 1)
            nc.gpsimd.iota(empty[:, :], [[1, 1]], base=2 * TOK, channel_multiplier=1,
                           allow_small_or_imprecise_dtypes=True).then_inc(set_up, 1)
            nc.gpsimd.memset(going[:, :, :], 1.0).then_inc(raw, 1)
            pool.wait_ge(raw, 2)
            nc.gpsimd.memset(going[:, :, 0:1], 0.0).then_inc(set_up, 1)
            nc.gpsimd.affine_select(out=later[:, :], in_=later[:, :], compare_op=ALU.is_gt, fill=-1.0, base=0,
                                    pattern=[[1, P]], channel_multiplier=-1).then_inc(set_up, 1)

        @block.scalar
        def _(act):
            act.wait_ge(gap_ok, 1)
            nc.scalar.activation(ex[:, :], gap[:, :], ACT.Exp).then_inc(exp_ok, 1)

        @block.vector
        def _(dve):
            n = [0]

            def did(ins):
                n[0] += 1
                ins.then_inc(st, 1)
                return ins

            dve.wait_ge(set_up, 8)
            nc.vector.tensor_tensor(gap[:, :], K.top[:, 1, :], K.top[:, 0, :], ALU.subtract).then_inc(gap_ok, 1)
            over_tiles = lambda x, n: x.rearrange("p (e a) -> p e a", a=1).broadcast_to([P, n, TT])
            for i in range(2):
                did(nc.vector.tensor_tensor(hot[i][:, :, :], over_tiles(expert[:, :], E),
                                            K.top_at[:, i:i + 1, :].broadcast_to([P, E, TT]), ALU.is_equal))
            dve.wait_ge(st, n[0])
            did(nc.vector.tensor_tensor(chosen[:, :, :], hot[0][:, :, :], hot[1][:, :, :], ALU.add))
            dve.wait_ge(st, n[0])
            flat = lambda x: x[:, :, :].rearrange("p e t -> p (e t)")
            nc.vector.tensor_tensor_scan(flat(upto), flat(going), flat(chosen), 0.0, ALU.mult,
                                         ALU.add).then_inc(sums, 1)
            dve.wait_ge(exp_ok, 1)
            did(nc.vector.tensor_scalar(ex1[:, :], ex[:, :], 1.0, None, ALU.add))
            dve.wait_ge(st, n[0])
            did(nc.vector.reciprocal(K.weight[:, 0, :], ex1[:, :]))
            dve.wait_ge(st, n[0])
            did(nc.vector.tensor_tensor(K.weight[:, 1, :], ex[:, :], K.weight[:, 0, :], ALU.mult))

            dve.wait_ge(ranks, 1)
            did(nc.vector.tensor_scalar(count[:, :], count_ps[:, 0:E], float(P - 1), None, ALU.add))
            dve.wait_ge(st, n[0])
            did(nc.vector.tensor_scalar(up[:, :], count[:, :], P.bit_length() - 1, None, ALU.arith_shift_right))
            dve.wait_ge(st, n[0])
            did(nc.vector.tensor_scalar(tiles[:, :], up[:, :], 1.0, None, ALU.max))
            dve.wait_ge(st, n[0])
            did(nc.vector.tensor_tensor_scan(ends[:, :], one[:, :], tiles[:, :], 0.0, ALU.mult, ALU.add))
            dve.wait_ge(st, n[0])
            did(nc.vector.tensor_tensor(start_at[:, :], ends[:, :], tiles[:, :], ALU.subtract))
            dve.wait_ge(st, n[0])
            did(nc.vector.scalar_tensor_tensor(out=K.span[:, :], in0=ends[:, :], scalar=float(SPAN), in1=start_at[:, :],
                                               op0=ALU.mult, op1=ALU.add))
            dve.wait_ge(st, n[0])
            did(nc.vector.tensor_scalar(start_at[:, :], start_at[:, :], float(P), None, ALU.mult))
            dve.wait_ge(st, n[0])
            for g in range(4):
                did(nc.vector.tensor_tensor(first[:, g * GE:(g + 1) * GE, :], rank_ps[g][:, :, :],
                                            over_tiles(start_at[:, g * GE:(g + 1) * GE], GE), ALU.add))
            dve.wait_ge(st, n[0])
            for i in range(2):
                did(nc.vector.tensor_tensor(picked[i][:, :, :], hot[i][:, :, :], first[:, :, :], ALU.mult))
            dve.wait_ge(st, n[0])
            for i in range(2):
                did(nc.vector.tensor_reduce(pos[:, i, :], picked[i][:, :, :].rearrange("p e t -> p t e"), AX_X,
                                            ALU.add))
            dve.wait_ge(st, n[0])
            did(nc.vector.tensor_copy(pos_i[:, :, :], pos[:, :, :]))
            dve.wait_ge(st, n[0])
            did(nc.vector.tensor_scalar(hi_i[:, :, :], pos_i[:, :, :], P.bit_length() - 1, None,
                                        ALU.arith_shift_right))
            did(nc.vector.tensor_scalar(lo_i[:, :, :], pos_i[:, :, :], P - 1, None, ALU.bitwise_and))
            dve.wait_ge(st, n[0])
            did(nc.vector.tensor_copy(hi[:, :], hi_i[:, :, :].rearrange("p s t -> p (s t)")))
            did(nc.vector.tensor_copy(lo[:, :], lo_i[:, :, :].rearrange("p s t -> p (s t)")))
            dve.wait_ge(st, n[0])
            did(nc.vector.tensor_tensor(entry[:, :], token[:, :, :].rearrange("p s t -> p (s t)"), lo[:, :],
                                        ALU.subtract))
            dve.wait_ge(st, n[0])
            with dve.Fori(0, 2 * TT // 4) as q:
                for u in range(4):
                    k = q * 4 + u
                    dve.wait_ge(used, k + 1)
                    settle(dve)
                    nc.vector.tensor_scalar(at_lo[u][:, :], place[:, 0:P], lo[:, bass.ds(k, 1)], None,
                                            ALU.is_equal).then_inc(marks, 1)
                    nc.vector.tensor_scalar(at_hi[u][:, :], place[:, :], hi[:, bass.ds(k, 1)], entry[:, bass.ds(k, 1)],
                                            ALU.is_equal, ALU.mult).then_inc(marks, 1)
            dve.wait_ge(tabled, 1)
            did(nc.vector.tensor_scalar(K.choice[:, :], table_ps[:, 0:MT + 1], empty[:, :], None, ALU.add))
            dve.wait_ge(st, n[0])
            did(nc.vector.tensor_scalar(K.table[:, :], K.choice[:, :], TOK - 1, None, ALU.bitwise_and))

        @block.tensor
        def _(pe):
            pe.sem_inc(used, 4)
            pe.wait_ge(set_up, 8)
            pe.wait_ge(sums, 1)
            nc.tensor.matmul(count_ps[:, 0:E], ones[:, :], upto[:, :, TT - 1:TT].rearrange("p e a -> p (e a)"),
                             start=True, stop=True)
            for g in range(4):
                es = slice(g * GE, (g + 1) * GE)
                nc.tensor.matmul(rank_ps[g][:, :, :], ones[:, :], upto[:, es, :], start=True, stop=False)
                m = nc.tensor.matmul(rank_ps[g][:, :, :], later[:, :], chosen[:, es, :], start=False, stop=True)
            m.then_inc(ranks, 1)

            def enter(k, u, start=False, stop=False):
                pe.wait_ge(marks, 2 * k + 2)
                m = nc.tensor.matmul(table_ps[:, 0:MT + 1], at_lo[u][:, :], at_hi[u][:, :], start=start, stop=stop)
                m.then_inc(used, 1)
                return m

            for u in range(4):
                enter(u, u, start=(u == 0))
            with pe.Fori(1, 2 * TT // 4 - 1) as q:
                for u in range(4):
                    enter(q * 4 + u, u)
            for u in range(4):
                m = enter(2 * TT - 4 + u, u, stop=(u == 3))
            pe.wait_ge(used, 4 + 2 * TT)
            pe.sem_inc(tabled, 1)


def load_weights(K, sp, e, r):
    one = lambda w: w[bass.ds(e, 1), :, :].rearrange("a (c p) f -> p (a c) f", p=P)
    for w, dram in zip(K.w[r], (K.w0_dram, K.w1_dram, K.wo_dram)):
        sp.dma_start(w[:, :, :], one(dram)).then_inc(K.w_in[r], 16)


def experts(K):
    nc, sem = K.nc, K.sem
    with ExitStack() as c:
        sb = lambda name, shape, dt=F32: c.enter_context(nc.sbuf_tensor(name, shape, dt))
        ps = lambda name, shape: c.enter_context(nc.psum_tensor(name, shape, F32))
        index = sb("mo_index", [P, 1], I32)
        index_ok = sem("mo_index_ok")
        to = sb("mo_to", [P, 1], I32)
        to_ok = sem("mo_to_ok")
        xg = sb("mo_xg", [P, D])
        xt = sb("mo_xt", [P, DC, P])
        silu = [sb(f"mo_silu{m}", [P, P]) for m in range(FC)]
        inter = [sb(f"mo_inter{m}", [P, P]) for m in range(FC)]
        o_sb = sb("mo_o", [P, D])
        h_ps = [ps(f"mo_h{m}", [P, 512]) for m in range(FC)]
        xt_ps = ps("mo_xt_ps", [P, 512])
        o_ps = ps("mo_o_ps", [P, 512])
        x_in = sem("mo_x_in")
        turned = sem("mo_turned")
        xt_ok = sem("mo_xt_ok")
        up_mm = sem("mo_up")
        silu_ok = sem("mo_silu_ok")
        inter_ok = sem("mo_inter_ok")
        down_mm = sem("mo_down")
        o_ok = sem("mo_o_ok")
        o_out = sem("mo_o_out")
        block = c.enter_context(nc.Block())

        def span(eng, e):
            packed = eng.value_load(K.span[0:1, bass.ds(e, 1)], min_val=SPAN, max_val=MT * SPAN + MT)
            return packed % SPAN, packed // SPAN

        @block.sync
        def _(sp):
            with sp.Fori(1, E // WRING) as q:
                for r in range(WRING):
                    _, end = span(sp, (q - 1) * WRING + r)
                    sp.wait_ge(down_mm, end * FC + FC)
                    settle(sp)
                    load_weights(K, sp, q * WRING + r, r)

        @block.gpsimd
        def _(pool):
            _, end = span(pool, E - 1)

            def gather(g):
                pool.wait_ge(turned, g + 1)
                settle(pool)
                nc.gpsimd.tensor_copy(index[:, :], K.table[:, bass.ds(g, 1)]).then_inc(index_ok, 1)
                pool.wait_ge(index_ok, g + 1)
                settle(pool)
                nc.gpsimd.indirect_dma_start(xg[:, :], None, K.xn_dram[:, :],
                                             bass.IndirectOffsetOnAxis(ap=index[:, :], axis=0)).then_inc(x_in, 16)

            def scatter(g):
                pool.wait_ge(o_ok, g + 2)
                settle(pool)
                nc.gpsimd.tensor_copy(to[:, :], K.choice[:, bass.ds(g, 1)]).then_inc(to_ok, 1)
                pool.wait_ge(to_ok, g + 1)
                settle(pool)
                nc.gpsimd.indirect_dma_start(K.outs_dram[:, :], bass.IndirectOffsetOnAxis(ap=to[:, :], axis=0),
                                             o_sb[:, :], None).then_inc(o_out, 16)

            gather(0)
            gather(1)
            with pool.Fori(2, end + 1) as g:
                gather(g)
                scatter(g - 2)
            scatter(end - 1)
            pool.wait_ge(o_out, end * 16)
            settle(pool)

        @block.tensor
        def _(pe):
            pe.sem_inc(down_mm, FC)
            pe.sem_inc(turned, 1)

            def turn(g):
                pe.wait_ge(x_in, g * 16 + 16)
                for c_ in range(DC):
                    m = nc.tensor.transpose(xt_ps[:, c_ * P:(c_ + 1) * P], xg[:, c_ * P:(c_ + 1) * P], K.ident[:, :])
                m.then_inc(turned, 1)

            def up(g, r, m):
                pe.wait_ge(inter_ok, g * FC + (m + 1))
                for i in range(2):
                    for c_ in range(DC):
                        ins = nc.tensor.matmul(h_ps[m][:, i * P:(i + 1) * P], K.w[r][i][:, c_, m * P:(m + 1) * P],
                                               xt[:, c_, :], start=(c_ == 0), stop=(c_ == DC - 1))
                ins.then_inc(up_mm, 1)

            def down(g, r, m):
                pe.wait_ge(inter_ok, g * FC + (FC + m + 1))
                if m == 0:
                    pe.wait_ge(o_ok, g + 1)
                nc.tensor.matmul(o_ps[:, 0:D], inter[m][:, :], K.w[r][2][:, m, :], start=(m == 0),
                                 stop=(m == FC - 1)).then_inc(down_mm, 1)

            turn(0)
            with pe.Fori(0, E // (2 * WRING)) as q:
                next_span = span(pe, q * 2 * WRING)
                for i in range(2 * WRING):
                    r = i % WRING
                    first, end = next_span
                    pe.wait_ge(K.w_in[r], q * 96 + (i // WRING + 1) * 48)
                    settle(pe)
                    with pe.Fori(first, end) as g:
                        pe.wait_ge(xt_ok, g + 1)
                        up(g, r, 0)
                        up(g, r, 1)
                        if i + 1 < 2 * WRING:
                            next_span = span(pe, q * 2 * WRING + i + 1)
                        up(g, r, 2)
                        down(g, r, 0)
                        up(g, r, 3)
                        down(g, r, 1)
                        turn(g + 1)
                        down(g, r, 2)
                        down(g, r, 3)

        @block.scalar
        def _(act):
            def activate(g, m):
                act.wait_ge(up_mm, g * FC + (m + 1))
                act.wait_ge(inter_ok, g * FC + (m + 1))
                nc.scalar.activation(silu[m][:, :], h_ps[m][:, 0:P], ACT.Silu).then_inc(silu_ok, 1)

            nc.scalar.preload_act_table(ACT.Silu)
            _, end = span(act, E - 1)
            with act.Fori(0, end) as g:
                for m in range(FC):
                    activate(g, m)

        @block.vector
        def _(dve):
            dve.sem_inc(inter_ok, FC)
            dve.sem_inc(o_ok, 1)

            def take_turned(g):
                dve.wait_ge(turned, g + 2)
                nc.vector.tensor_copy(xt[:, :, :], xt_ps[:, 0:D].rearrange("p (c t) -> p c t", c=DC)
                                      ).then_inc(xt_ok, 1)

            def tile(g):
                for m in range(FC):
                    dve.wait_ge(silu_ok, g * FC + (m + 1))
                    dve.wait_ge(down_mm, g * FC + (m + 1))
                    nc.vector.tensor_tensor(inter[m][:, :], silu[m][:, :], h_ps[m][:, P:2 * P],
                                            ALU.mult).then_inc(inter_ok, 1)
                take_turned(g + 1)
                dve.wait_ge(down_mm, g * FC + 2 * FC)
                if not isinstance(g, int):
                    dve.wait_ge(o_out, g * 16)
                nc.vector.tensor_copy(o_sb[:, :], o_ps[:, 0:D]).then_inc(o_ok, 1)

            take_turned(0)
            _, end = span(dve, E - 1)
            tile(0)
            with dve.Fori(1, end) as g:
                tile(g)


def combine(K):
    nc, sem = K.nc, K.sem
    RING, G = 4, 4
    with ExitStack() as c:
        got = [[c.enter_context(nc.sbuf_tensor(f"co_got{u}_{i}", [P, G, D], F32)) for i in range(2)]
               for u in range(RING)]
        got_in = [sem(f"co_got_in{u}") for u in range(RING)]
        added = sem("co_added")
        out = sem("co_out")
        block = c.enter_context(nc.Block())
        rows = lambda k, first=0: bass.ds(first + k * G * P, G * P)

        @block.sync
        def _(sp):
            for k in range(TT // G):
                if k >= RING:
                    sp.wait_ge(added, (k - RING + 1) * 2 * G)
                for i in range(2):
                    sp.dma_start(got[k % RING][i][:, :, :],
                                 K.outs_dram[rows(k, i * TOK), :].rearrange("(t p) d -> p t d", p=P)
                                 ).then_inc(got_in[k % RING], 16)

        @block.vector
        def _(dve):
            for k in range(TT // G):
                u = k % RING
                dve.wait_ge(got_in[u], k // RING * 32 + 32)
                for i in range(2):
                    if i:
                        dve.wait_ge(added, k * 2 * G + G)
                    for g in range(G):
                        t = k * G + g
                        nc.vector.scalar_tensor_tensor(out=K.x[:, t, :], in0=got[u][i][:, g, :],
                                                       scalar=K.weight[:, i, t:t + 1], in1=K.x[:, t, :],
                                                       op0=ALU.mult, op1=ALU.add).then_inc(added, 1)

        @block.scalar
        def _(act):
            for k in range(TT // G):
                act.wait_ge(added, (k + 1) * 2 * G)
                act.dma_start(K.out_dram[rows(k), :].rearrange("(t p) d -> p t d", p=P),
                              K.x[:, k * G:(k + 1) * G, :]).then_inc(out, 16)
            act.wait_ge(out, TT // G * 16)


def build(nc, x, ctx_in, a_log, w_delta, w_dt, b_dt, w_b, w_c, d_skip, gate, w0, w1, wo, out):
    K = Chip()
    K.nc = nc
    with ExitStack() as ctx:
        K.ctx = ctx
        sb = lambda name, shape, dt=F32: ctx.enter_context(nc.sbuf_tensor(name, shape, dt))
        K.sem = lambda name: ctx.enter_context(nc.semaphore(name))
        K.dist_dram = nc.dram_tensor("dist", (B, L, L), F32, kind="Internal").ap()
        K.xn_dram = nc.dram_tensor("xn", (TOK, D), F32, kind="Internal").ap()
        K.outs_dram = nc.dram_tensor("outs", (2 * TOK + P, D), F32, kind="Internal").ap()
        K.x_dram = x.rearrange("b l d -> (b l) d")
        K.ctx_dram = ctx_in
        K.a_log_dram, K.w_delta_dram, K.w_dt_dram, K.b_dt_dram = a_log, w_delta, w_dt, b_dt
        K.w_b_dram, K.w_c_dram, K.d_skip_dram, K.gate_dram = w_b, w_c, d_skip, gate
        K.w0_dram, K.w1_dram, K.wo_dram = w0, w1, wo
        K.out_dram = out.rearrange("b l d -> (b l) d")

        K.x = sb("x", [P, TT, D])
        K.ident = sb("ident", [P, P])
        K.gate = sb("gate", [P, DC, E])
        K.hi = sb("hi", [P, 2, B])
        K.lo = sb("lo", [P, 2, B])

        K.codes = sb("codes", [P, SEG, BR, 2, SW], F16)
        K.cx = K.codes[:, :, :, :, :].rearrange("p s i a j -> p (s i a j)").bitcast(F32).rearrange(
            "p (t d) -> p t d", d=D)
        with ExitStack() as c_wave:
            K.wave = c_wave.enter_context(nc.sbuf_tensor("wave", [P, STEPS * SW], F32))
            with ExitStack() as ssm:
                sb2 = lambda name, shape, dt=F32: ssm.enter_context(nc.sbuf_tensor(name, shape, dt))
                K.rstd = sb2("rstd", [P, TT])
                K.nmr = sb2("nmr", [P, TT])
                K.a_neg = sb2("a_neg", [P, DC, N])
                K.w_delta = sb2("w_delta", [P, DC, R])
                K.w_dt = sb2("w_dt", [R, D])
                K.b_dt = sb2("b_dt", [P, DC])
                K.d_skip = sb2("d_skip", [P, DC])
                K.w_bc = sb2("w_bc", [P, DC, 2 * N])
                K.xt = sb2("xt", [P, DC, TOK])
                K.delta = sb2("delta", [P, DC, TOK])
                K.dx = K.wave[:, 0:DC * TOK].rearrange("p (c t) -> p c t", c=DC)
                spare = K.codes[:, :, :, :, :].rearrange("p s i a j -> p (s i a j)").bitcast(BF16)
                K.bc3 = spare[0:6 * N, 0:TOK]
                K.bc_sel = spare[0:6 * N, TOK:TOK + 2 * N * P].rearrange("p (m q) -> p m q", q=P)
                run(K, load_and_constants, prepare, scan_states, distances)
            run(K, wave)
        run(K, trace_back)
        sb3 = lambda name, shape, dt=F32: ctx.enter_context(nc.sbuf_tensor(name, shape, dt))
        K.w = [[sb3(f"w0_{r}", [P, DC, F]), sb3(f"w1_{r}", [P, DC, F]), sb3(f"wo_{r}", [P, FC, D])]
               for r in range(WRING)]
        K.w_in = [K.sem(f"w_in{r}") for r in range(WRING)]
        K.top = sb3("top", [P, 2, TT])
        K.top_at = sb3("top_at", [P, 2, TT])
        K.weight = sb3("weight", [P, 2, TT])
        K.span = sb3("span", [P, E], I32)
        K.choice = sb3("choice", [P, MT + 1], I32)
        K.table = sb3("table", [P, MT + 1], I32)
        run(K, expand)
        run(K, route, experts, combine)


_INS = ['x', 'ctx_1024', 'L0_attn_A_log', 'L0_attn_W_delta', 'L0_attn_W_dt', 'L0_attn_b_dt', 'L0_attn_W_B',
        'L0_attn_W_C', 'L0_attn_D', 'L0_ffn_gate_kernel', 'L0_ffn_w0', 'L0_ffn_w1', 'L0_ffn_wo']
_OUTS = [((B, L, D), 'float32')]


def kernel(**inputs):
    import numpy as _np
    import concourse.bacc as _bacc
    from concourse import mybir as _mybir
    from concourse.bass_utils import run_bass_kernel_spmd as _run

    nc = _bacc.Bacc("TRN2", target_bir_lowering=False, num_devices=1)
    arrays, args = {}, []
    for name in _INS:
        a = _np.ascontiguousarray(inputs[name])
        arrays[f"in_{name}_dram"] = a
        args.append(nc.dram_tensor(f"in_{name}_dram", a.shape, _mybir.dt.from_np(a.dtype), kind="ExternalInput").ap())
    for i, (shape, dtype) in enumerate(_OUTS):
        dt = _mybir.dt.from_np(_np.dtype(dtype))
        args.append(nc.dram_tensor(f"out_{i}_dram", shape, dt, kind="ExternalOutput").ap())
    build(nc, *args)
    r = _run(nc, [arrays], core_ids=[0])
    got = tuple(r.results[0][f"out_{i}_dram"] for i in range(len(_OUTS)))
    return got[0]
```
